# Optimizing a Trainium2 kernel written in Bass

```python
import numpy as np
import jax
import jax.numpy as jnp

def _softmax(x, axis=-1):
    return jax.nn.softmax(x, axis=axis)

def _gelu(x):
    return jax.nn.gelu(x, approximate=True)

def _silu(x):
    return jax.nn.silu(x)

def _sigmoid(x):
    return jax.nn.sigmoid(x)

def _layernorm(x, axis=-1, eps=1e-05):
    m = jnp.mean(x, axis=axis, keepdims=True)
    v = jnp.var(x, axis=axis, keepdims=True)
    return (x - m) / jnp.sqrt(v + eps)

def _scatter_add(tgt, idx, src, axis=0):
    return tgt.at[idx].add(src)

def _segment_sum(src, seg, n):
    return jax.ops.segment_sum(src, seg, n)
kernel_name = 'mk_adaln_ffn_d2_seqx_r8_02f81f'

def setup_inputs(seed: int=0):
    np.random.seed(seed)
    _w = jnp.asarray

    def _rec_inputs():
        import jax
        import jax.numpy as jnp
        _rk = jax.random.key(seed)
        x = -7.109e-05 + 0.9999 * jax.random.normal(jax.random.fold_in(_rk, 1), (8, 128, 512), jnp.float32)
        _lenS = 128 - jax.random.randint(jax.random.fold_in(_rk, 7), (8,), 0, max(1, 128 // 4) + 1, jnp.int32)
        _lenS2 = 128 - jax.random.randint(jax.random.fold_in(_rk, 8), (8,), 0, max(1, 128 // 4) + 1, jnp.int32)
        itok_B_0_4 = jax.random.randint(jax.random.fold_in(_rk, 11), (8,), 0, 5, jnp.int32)
        itok_B_0_15 = jax.random.randint(jax.random.fold_in(_rk, 12), (8,), 0, 16, jnp.int32)
        return (x, itok_B_0_4, itok_B_0_15)
    x, itok_B_0_4, itok_B_0_15 = _rec_inputs()

    def _L0_cond_setup():
        import jax, jax.numpy as jnp
        import numpy as np
        B, S, D_IN, D_OUT = (8, 256, 512, 512)
        R, NUM_LABELERS = (32, 5)
        LORA_SCALING = 16 / 32
        key = jax.random.key(seed)
        k1, k2, k3, k4, k5, k6 = jax.random.split(key, 6)
        inp = {'input': jax.random.normal(k1, (B, S, D_IN), dtype=jnp.float32), 'weight': jax.random.normal(k2, (D_OUT, D_IN), dtype=jnp.float32) * 0.02, 'bias': jax.random.normal(k3, (D_OUT,), dtype=jnp.float32) * 0.02, 'lora_A': jax.random.normal(k4, (NUM_LABELERS, D_IN, R), dtype=jnp.float32) * 0.02, 'lora_B': jax.random.normal(k5, (D_OUT, R), dtype=jnp.float32) * 0.02, 'labeler_index': jax.random.randint(k6, (B,), 0, NUM_LABELERS, dtype=jnp.int64) if jax.config.jax_enable_x64 else jax.random.randint(k6, (B,), 0, NUM_LABELERS, dtype=jnp.int32)}
        return inp
    _L0_cond_all = _L0_cond_setup()
    _L0_cond_in = {k: v for k, v in _L0_cond_all.items() if k in ('weight', 'bias', 'lora_A', 'lora_B')}
    del _L0_cond_all

    def _L0_ffn_setup():
        import jax, jax.numpy as jnp
        import numpy as np
        R = 16
        LORA_ALPHA = 16
        SCALING = LORA_ALPHA / R
        key = jax.random.key(seed)
        kx, kr, ka = jax.random.split(key, 3)
        B, S, D, DO, E = (4, 256, 512, 512, 8)
        x = jax.random.normal(kx, (B, S, D), dtype=jnp.float32)
        bound_r = 1.0 / np.sqrt(D)
        route_w = jax.random.uniform(kr, (E, D), jnp.float32, -bound_r, bound_r)
        bound_a = 1.0 / np.sqrt(D)
        A = jax.random.uniform(ka, (E, R, D), jnp.float32, -bound_a, bound_a)
        kb = jax.random.fold_in(key, 7)
        Bw = jax.random.normal(kb, (E, DO, R), dtype=jnp.float32) * 0.02
        return {'x': x, 'route_w': route_w, 'A': A, 'Bw': Bw}
    _L0_ffn_all = _L0_ffn_setup()
    _L0_ffn_in = {k: v for k, v in _L0_ffn_all.items() if k in ('route_w', 'A', 'Bw')}
    del _L0_ffn_all

    def _L1_cond_setup():
        import jax, jax.numpy as jnp
        import numpy as np
        SCALING = 16.0 / 16
        key = jax.random.key(seed)
        k1, k2, k3, k4, k5 = jax.random.split(key, 5)
        B, S, D_IN, D_OUT, R, N_ADPT = (8, 256, 512, 512, 16, 16)
        x = jax.random.normal(k1, (B, S, D_IN), dtype=jnp.float32)
        adapter_indices = jax.random.randint(k2, (B,), 0, N_ADPT, dtype=jnp.int32)
        W = jax.random.normal(k3, (D_IN, D_OUT), dtype=jnp.float32) * 0.02
        lora_A = jax.random.normal(k4, (N_ADPT, D_IN, R), dtype=jnp.float32) * 0.02
        lora_B = jax.random.normal(k5, (N_ADPT, R, D_OUT), dtype=jnp.float32) * 0.02
        return {'x': x, 'adapter_indices': adapter_indices, 'W': W, 'lora_A': lora_A, 'lora_B': lora_B}
    _L1_cond_all = _L1_cond_setup()
    _L1_cond_in = {k: v for k, v in _L1_cond_all.items() if k in ('W', 'lora_A', 'lora_B')}
    del _L1_cond_all

    def _L1_ffn_setup():
        import jax, jax.numpy as jnp
        import numpy as np
        D_IN = 512
        D_OUT = 512
        RANK = 16
        NUM_EXPERTS = 8
        TOP_K = 2
        SCALING = 32.0 / RANK
        key = jax.random.key(seed)
        ks = jax.random.split(key, 6)
        x = jax.random.normal(ks[0], (4, 256, D_IN), dtype=jnp.float32)
        W_base = jax.random.normal(ks[1], (D_OUT, D_IN), dtype=jnp.float32) * (1.0 / np.sqrt(D_IN))
        b_base = jax.random.normal(ks[2], (D_OUT,), dtype=jnp.float32) * 0.01
        W_router = jax.random.normal(ks[3], (NUM_EXPERTS, D_IN), dtype=jnp.float32) * 0.01
        A_stack = jax.random.uniform(ks[4], (NUM_EXPERTS, RANK, D_IN), dtype=jnp.float32, minval=-1.0, maxval=1.0) * (1.0 / np.sqrt(D_IN))
        B_stack = jax.random.normal(ks[5], (NUM_EXPERTS, D_OUT, RANK), dtype=jnp.float32) * 0.02
        return {'x': x, 'W_base': W_base, 'b_base': b_base, 'W_router': W_router, 'A_stack': A_stack, 'B_stack': B_stack}
    _L1_ffn_all = _L1_ffn_setup()
    _L1_ffn_in = {k: v for k, v in _L1_ffn_all.items() if k in ('W_base', 'b_base', 'W_router', 'A_stack', 'B_stack')}
    del _L1_ffn_all
    return {'x': x, 'itok_B_0_4': itok_B_0_4, 'itok_B_0_15': itok_B_0_15, 'L0_cond_weight': _L0_cond_in['weight'], 'L0_cond_bias': _L0_cond_in['bias'], 'L0_cond_lora_A': _L0_cond_in['lora_A'], 'L0_cond_lora_B': _L0_cond_in['lora_B'], 'L0_ffn_route_w': _L0_ffn_in['route_w'], 'L0_ffn_A': _L0_ffn_in['A'], 'L0_ffn_Bw': _L0_ffn_in['Bw'], 'L1_cond_W': _L1_cond_in['W'], 'L1_cond_lora_A': _L1_cond_in['lora_A'], 'L1_cond_lora_B': _L1_cond_in['lora_B'], 'L1_ffn_W_base': _L1_ffn_in['W_base'], 'L1_ffn_b_base': _L1_ffn_in['b_base'], 'L1_ffn_W_router': _L1_ffn_in['W_router'], 'L1_ffn_A_stack': _L1_ffn_in['A_stack'], 'L1_ffn_B_stack': _L1_ffn_in['B_stack']}

def reference(x, itok_B_0_4, itok_B_0_15, L0_cond_weight, L0_cond_bias, L0_cond_lora_A, L0_cond_lora_B, L0_ffn_route_w, L0_ffn_A, L0_ffn_Bw, L1_cond_W, L1_cond_lora_A, L1_cond_lora_B, L1_ffn_W_base, L1_ffn_b_base, L1_ffn_W_router, L1_ffn_A_stack, L1_ffn_B_stack):
    import jax
    import jax.numpy as jnp

    def _L0_cond_ref(input, weight, bias, lora_A, lora_B, labeler_index):
        import jax, jax.numpy as jnp
        import numpy as np
        B, S, D_IN, D_OUT = (8, 256, 512, 512)
        R, NUM_LABELERS = (32, 5)
        LORA_SCALING = 16 / 32
        base = jnp.einsum('bsi,oi->bso', input, weight) + bias
        labelers_A = lora_A[labeler_index]
        ax = jnp.einsum('bsi,bir->bsr', input, labelers_A)
        delta = jnp.einsum('bsr,or->bso', ax, lora_B)
        return base + delta * LORA_SCALING

    def _L0_ffn_ref(x, route_w, A, Bw):
        import jax, jax.numpy as jnp
        import numpy as np
        R = 16
        LORA_ALPHA = 16
        SCALING = LORA_ALPHA / R
        logits = jnp.einsum('bsd,ed->bse', x, route_w)
        topk_v, topk_idx = jax.lax.top_k(logits, 1)
        E = logits.shape[-1]
        route_weight = jax.nn.one_hot(topk_idx[..., 0], E, dtype=logits.dtype) * topk_v
        h = jnp.einsum('bsd,erd->bser', x, A)
        wh = route_weight[..., None] * h
        out = jnp.einsum('bser,eor->bso', wh, Bw) * SCALING
        return out

    def _L1_cond_ref(x, adapter_indices, W, lora_A, lora_B):
        import jax, jax.numpy as jnp
        import numpy as np
        SCALING = 16.0 / 16
        base_out = jnp.einsum('bsi,io->bso', x, W)
        A = lora_A[adapter_indices]
        Bm = lora_B[adapter_indices]
        xr = jnp.einsum('bsi,bir->bsr', x, A)
        lora_out = jnp.einsum('bsr,bro->bso', xr, Bm)
        return base_out + lora_out * SCALING

    def _L1_ffn_ref(x, W_base, b_base, W_router, A_stack, B_stack):
        import jax, jax.numpy as jnp
        import numpy as np
        D_IN = 512
        D_OUT = 512
        RANK = 16
        NUM_EXPERTS = 8
        TOP_K = 2
        SCALING = 32.0 / RANK
        orig_shape = x.shape
        xf = x.reshape(-1, D_IN)
        logits = xf @ W_router.T
        probs = jax.nn.softmax(logits, axis=-1)
        topk_p, topk_i = jax.lax.top_k(probs, TOP_K)
        topk_p = topk_p / jnp.sum(topk_p, axis=-1, keepdims=True)
        combine = jnp.sum(jax.nn.one_hot(topk_i, NUM_EXPERTS, dtype=xf.dtype) * topk_p[..., None], axis=1)
        h = jnp.einsum('nd,erd->ner', xf, A_stack)
        h = h * combine[..., None]
        lora_out = jnp.einsum('ner,eor->no', h, B_stack) * SCALING
        base_out = xf @ W_base.T + b_base
        out = base_out + lora_out
        return out.reshape(orig_shape[:-1] + (D_OUT,))
    x = x + _L0_ffn_ref(_L0_cond_ref(x, L0_cond_weight, L0_cond_bias, L0_cond_lora_A, L0_cond_lora_B, itok_B_0_4), L0_ffn_route_w, L0_ffn_A, L0_ffn_Bw)
    x = x + _L1_ffn_ref(_L1_cond_ref(x, itok_B_0_15, L1_cond_W, L1_cond_lora_A, L1_cond_lora_B), L1_ffn_W_base, L1_ffn_b_base, L1_ffn_W_router, L1_ffn_A_stack, L1_ffn_B_stack)
    return x

_drawn_inputs = setup_inputs


def setup_inputs(seed=0):
    import zlib

    import numpy as np

    out = dict(_drawn_inputs(seed))
    spreads = {}
    factors = {'L0_cond_weight': 5.015,
     'L0_cond_bias': 8.0,
     'L0_cond_lora_A': 8.0,
     'L0_cond_lora_B': 8.0,
     'L0_ffn_route_w': 4.521,
     'L0_ffn_A': 4.28,
     'L0_ffn_Bw': 4.299,
     'L1_ffn_b_base': 200.0}
    for name, (base, spread) in spreads.items():
        noise = np.random.default_rng([zlib.crc32(name.encode()), seed]).standard_normal(out[name].shape)
        drawn = base * np.exp(spread * noise) if base else spread * noise
        out[name] = jnp.asarray(drawn.astype(out[name].dtype))
    for name, factor in factors.items():
        out[name] = (out[name] * factor).astype(out[name].dtype)
    return out
```

```python
from contextlib import ExitStack

import concourse.bass as bass
from concourse import mybir

F32 = mybir.dt.float32
F32R = mybir.dt.float32r
I32 = mybir.dt.int32
U32 = mybir.dt.uint32
ALU = mybir.AluOpType
ACT = mybir.ActivationFunctionType

P = 128
HIGH, LOW = 0, 1
PASSES = ((HIGH, HIGH), (HIGH, LOW), (LOW, HIGH))


def adaln_ffn_kernel(nc, x, label0, label1, w0, bias0, lora_a0, lora_b0, route0, exp_a0, exp_b0,
                     w1, lora_a1, lora_b1, w_base, b_base, route1, exp_a1, exp_b1, out):
    B, S, D = x.shape
    L0, _, R0 = lora_a0.shape
    L1, _, R1 = lora_a1.shape
    E, RE, _ = exp_a0.shape
    KC = D // P
    ER = E * RE
    SIDE = ER + E
    N0 = SIDE + R0
    U0 = R0 + 1
    HB = D // 2
    NB = SIDE + HB
    NCAT = SIDE + D
    WB = R1 + NB + R1
    BR = B * R1
    BLOCKS = ((0, NB), (NB, NCAT))
    PAIRS = B // 2
    SCALE0 = 16 / 32
    SCALE_FFN1 = 32.0 / 16
    assert S == P and ER == P and BR == P and D % P == 0 and R1 == RE

    with ExitStack() as ctx:
        def sb(name, shape, dt=F32):
            return ctx.enter_context(nc.sbuf_tensor(name, shape, dt))

        def sem(name):
            return ctx.enter_context(nc.semaphore(name))

        ident = sb("ident", [P, P])
        diag = sb("diag", [P, NCAT + KC - 1])
        own_batch = sb("own_batch", [P, B])
        expert_no = sb("expert_no", [P, E])
        exp_a0_n = sb("exp_a0_n", [ER, D])
        route0_n = sb("route0_n", [E, D])
        w0_n = sb("w0_n", [P, KC, D])
        lora_b0_n = sb("lora_b0_n", [P, KC, U0])
        bias0_n = sb("bias0_n", [P, KC])
        exp_b0_n = sb("exp_b0_n", [P, E, KC * RE])
        w_base_n = sb("w_base_n", [P, KC, D])
        exp_a1_n = sb("exp_a1_n", [ER, D])
        route1_n = sb("route1_n", [E, D])
        w1_n = sb("w1_n", [P, KC, D])
        exp_b1_n = sb("exp_b1_n", [P, E, KC * RE])
        b_base_all = sb("b_base_all", [P, D])
        labels = sb("labels", [1, 2, B], I32)
        lora_a0_g = sb("lora_a0_g", [P, B, KC, R0])
        lora_a1_g = sb("lora_a1_g", [P, B, KC, R1])
        lora_b1_g = sb("lora_b1_g", [BR, D])
        exp_b0_c = sb("exp_b0_c", [P, KC, ER])
        exp_b1_c = sb("exp_b1_c", [P, KC, ER])
        cat0_t = sb("cat0_t", [P, KC, SIDE])
        m0 = [sb(f"m0_{s}", [P, KC, N0]) for s in range(2)]
        g0 = sb("g0", [U0, SIDE])
        exp_b0_t = [sb(f"exp_b0_t{h}", [ER, KC, P], F32R) for h in range(2)]
        lora_b1_t = [sb(f"lora_b1_t{h}", [P, KC, BR], F32R) for h in range(2)]
        cat1_t = [sb(f"cat1_t{h}", [P, KC, NCAT], F32R) for h in range(2)]
        w1_t = [sb(f"w1_t{h}", [P, 2, KC, P], F32R) for h in range(2)]
        g1 = [sb(f"g1_{h}", [BR, NCAT], F32R) for h in range(2)]
        m1_f = sb("m1_f", [P, 2, NCAT])
        m1_b = [sb(f"m1_b{h}", [P, KC, WB], F32R) for h in range(2)]
        m1_a = [sb(f"m1_a{h}", [P, KC, HB], F32R) for h in range(2)]
        exp_b1_t = [sb(f"exp_b1_t{h}", [ER, P, KC], F32R) for h in range(2)]
        x_in = sb("x_in", [P, 2, D])
        x_t = sb("x_t", [P, KC, 2, P])
        x1_f = sb("x1_f", [P, KC, 2, P])
        x1_t = [sb(f"x1_t{h}", [P, KC, 2, P], F32R) for h in range(2)]
        u0 = sb("u0", [P, 2, U0])
        u0_t = sb("u0_t", [U0, 2, P])
        top0 = sb("top0", [P, 2, 8])
        top0_at = sb("top0_at", [P, 2, 8], U32)
        gate0 = sb("gate0", [P, 2, E])
        gated0 = sb("gated0", [P, 2, ER])
        gated0_t = [sb(f"gated0_t{h}", [ER, 2, P], F32R) for h in range(2)]
        u1 = sb("u1", [P, 2, B, R1])
        u1_t = [sb(f"u1_t{h}", [BR, 2, P], F32R) for h in range(2)]
        top1 = sb("top1", [P, 2, 8])
        top1_at = sb("top1_at", [P, 2, 8], U32)
        below = sb("below", [P, 2, E])
        expo = sb("expo", [P, 2, E])
        first = sb("first", [P, 2, E])
        chosen = sb("chosen", [P, 2, E])
        weight = sb("weight", [P, 2, E])
        total = sb("total", [P, 2])
        inverse = sb("inverse", [P, 2])
        gated1 = sb("gated1", [P, 2, ER])
        gated1_t = [sb(f"gated1_t{h}", [ER, 2, P], F32R) for h in range(2)]
        y = sb("y", [P, 2, D])

        bank_x = ctx.enter_context(nc.psum_tensor("bank_x", [P, 512], F32))
        bank_l0 = [ctx.enter_context(nc.psum_tensor(f"bank_l0_{s}", [P, 512], F32)) for s in range(2)]
        bank_small = ctx.enter_context(nc.psum_tensor("bank_small", [P, 512], F32))
        acc = [ctx.enter_context(nc.psum_tensor(f"acc_{s}", [P, 1024], F32)) for s in range(2)]
        banks = [bank_x[:, :], bank_l0[0][:, :], bank_l0[1][:, :], bank_small[:, :],
                 acc[0][:, 0:512], acc[0][:, 512:1024], acc[1][:, 0:512], acc[1][:, 512:1024]]

        U0_T, GATED0_T = N0, N0 + P
        SIDE_AT = (R1, 0)
        U1_AT = (0, NB)
        A1_AT = (0, R1 + NB)

        def b_bank(s, a, b):
            return acc[s][:, a:b]

        def base_part(s):
            at = SIDE_AT[s] + SIDE
            w = 512 - at
            return acc[s][:, at:at + 2 * w].rearrange("p (a b) -> p a b", a=2)[:, :, 0:HB]

        labels_in, x_loaded, a0_gathered, b1_gathered, a1_gathered = (
            sem(n) for n in ("labels_in", "x_loaded", "a0_gathered", "b1_gathered", "a1_gathered"))
        exp_a0_in, w0_in, lora_b0_in, exp_b0_in = (sem(n) for n in ("exp_a0_in", "w0_in", "lora_b0_in", "exp_b0_in"))
        w_base_in, exp_a1_in, w1_in, exp_b1_in, b_base_in = (
            sem(n) for n in ("w_base_in", "exp_a1_in", "w1_in", "exp_b1_in", "b_base_in"))
        const_step, exp_b_split, bias_placed, m0_copied, a0_placed, a1_high, a1_placed = (
            sem(n) for n in ("const_step", "exp_b_split", "bias_placed", "m0_copied", "a0_placed", "a1_high", "a1_placed"))
        stored = [sem(f"stored_{s}") for s in range(2)]
        prep_filled, prep_high, prep_low, m1_low = (sem(n) for n in ("prep_filled", "prep_high", "prep_low", "m1_low"))
        xt_filled, xt_copied, l0_scored, u0_copied, u0t_filled, u0t_copied, l0_ready = (
            sem(n) for n in ("xt_filled", "xt_copied", "l0_scored", "u0_copied", "u0t_filled", "u0t_copied", "l0_ready"))
        gated0_ready, gated0t_filled, gated0t_high, gated0t_low, x1_filled, x1_summed, x1_high, x1_low = (
            sem(n) for n in ("gated0_ready", "gated0t_filled", "gated0t_high", "gated0t_low", "x1_filled", "x1_summed",
                             "x1_high", "x1_low"))
        side_scored, base_scored, u1_copied, u1t_filled, u1t_high, u1t_low, l1_ready = (
            sem(n) for n in ("side_scored", "base_scored", "u1_copied", "u1t_filled", "u1t_high", "u1t_low", "l1_ready"))
        below_ready, expo_ready, gated1_ready, gated1t_filled, gated1t_high, gated1t_low, y_filled, y_ready, dve_step = (
            sem(n) for n in ("below_ready", "expo_ready", "gated1_ready", "gated1t_filled", "gated1t_high", "gated1t_low",
                             "y_filled", "y_ready", "dve_step"))

        (F_A0, F_ROUTE0, F_B0, F_M0, F_M0_G0, F_LORA_B1, F_A1, F_ROUTE1), F_BASE = range(8), 8
        F_G1, F_B1 = F_BASE + KC, F_BASE + KC + 2
        F_W1 = [F_B1 + 1] + [F_B1 + 3 * c - 1 for c in range(1, KC)]
        F_M1 = [F_B1 + 3 * c + 3 for c in range(KC - 1)] + [F_B1 + 3 * KC - 1]
        FILLS = F_B1 + 1 + 3 * KC
        NOT_ON_ACT, NOT_ON_DVE = (F_ROUTE0,), (F_A0, F_M0, F_M0_G0)

        def high_of(n):
            return prep_high, sum(k not in NOT_ON_ACT for k in range(n + 1))

        def low_of(n):
            return prep_low, sum(k not in NOT_ON_DVE for k in range(n + 1))

        def emptied(n):
            return high_of(n) if n in NOT_ON_DVE else low_of(n)

        block = ctx.enter_context(nc.Block())

        @block.sync
        def _(sp):
            sp.dma_start(labels[0:1, 0, :], label0.rearrange("(a n) -> a n", a=1)).then_inc(labels_in, 16)
            sp.dma_start(labels[0:1, 1, :], label1.rearrange("(a n) -> a n", a=1)).then_inc(labels_in, 16)
            sp.dma_start(exp_a0_n[:, :], exp_a0.rearrange("e r d -> (e r) d")).then_inc(exp_a0_in, 16)
            sp.dma_start(route0_n[:, :], route0).then_inc(exp_a0_in, 16)
            sp.dma_start(w0_n[:, :, :], w0.rearrange("(p k) i -> p k i", k=KC)).then_inc(w0_in, 16)
            sp.dma_start(bias0_n[:, :], bias0.rearrange("(p k) -> p k", k=KC)).then_inc(lora_b0_in, 16)
            sp.dma_start(lora_b0_n[:, :, 0:R0], lora_b0.rearrange("(p k) r -> p k r", k=KC)).then_inc(lora_b0_in, 16)
            sp.dma_start(exp_b0_n[:, :, :], exp_b0.rearrange("e (p c) r -> p e (c r)", c=KC)).then_inc(exp_b0_in, 16)
            sp.dma_start(w_base_n[:, :, :], w_base.rearrange("(j p) o -> p j o", p=P)).then_inc(w_base_in, 16)
            sp.dma_start(exp_a1_n[:, :], exp_a1.rearrange("e r d -> (e r) d")).then_inc(exp_a1_in, 16)
            sp.dma_start(route1_n[:, :], route1).then_inc(exp_a1_in, 16)
            sp.dma_start(w1_n[:, :, :], w1.rearrange("(p c) o -> p c o", c=KC)).then_inc(w1_in, 16)
            sp.dma_start(exp_b1_n[:, :, :], exp_b1.rearrange("e (p c) r -> p e (c r)", c=KC)).then_inc(exp_b1_in, 16)
            sp.dma_start(x_in[:, :, :], x[0:2].rearrange("b s d -> s b d")).then_inc(x_loaded, 16)
            sp.dma_start(b_base_all[:, :], b_base.rearrange("(a n) -> a n", a=1).to_broadcast([P, D])).then_inc(b_base_in, 16)
            sp.wait_ge(labels_in, 32)
            with sp.Fori(0, B) as b:
                n = sp.value_load(labels[0:1, 0, bass.ds(b, 1)], min_val=0, max_val=L0 - 1)
                sp.dma_start(lora_a0_g[:, bass.ds(b, 1), :, :],
                             lora_a0[bass.ds(n, 1)].rearrange("a (p c) r -> p a c r", c=KC)).then_inc(a0_gathered, 16)
            for b in range(B):
                m = sp.value_load(labels[0:1, 1, b:b + 1], min_val=0, max_val=L1 - 1)
                sp.dma_start(lora_b1_g[b * R1:(b + 1) * R1, :],
                             lora_b1[bass.ds(m, 1)].rearrange("a r o -> (a r) o")).then_inc(b1_gathered, 16)
                sp.dma_start(lora_a1_g[:, b:b + 1, :, :],
                             lora_a1[bass.ds(m, 1)].rearrange("a (p c) r -> p a c r", c=KC)).then_inc(a1_gathered, 16)

            def store(t, side):
                sp.wait_ge(y_ready, t + 1)
                sp.dma_start(out[bass.ds(t, 1)].rearrange("b s d -> (b s) d"), y[:, side, :]).then_inc(stored[side], 16)

            for p in range(PAIRS):
                if p + 1 < PAIRS:
                    sp.wait_ge(xt_filled, 2 * p + 2)
                    sp.dma_start(x_in[:, :, :], x[bass.ds(2 * p + 2, 2)].rearrange("b s d -> s b d")).then_inc(x_loaded, 16)
                store(2 * p, 0)
                store(2 * p + 1, 1)
            for side in range(2):
                sp.wait_ge(stored[side], 16 * PAIRS)

        @block.gpsimd
        def _(pool):
            pool.memset(ident[:, :], 0.0).then_inc(const_step, 1)
            pool.memset(diag[:, :], 0.0).then_inc(const_step, 1)
            pool.memset(own_batch[:, :], 1.0).then_inc(const_step, 1)
            pool.wait_ge(const_step, 1)
            pool.affine_select(out=ident[:, :], in_=ident[:, :], compare_op=ALU.not_equal, fill=1.0, base=0,
                               pattern=[[-1, P]], channel_multiplier=1).then_inc(const_step, 1)
            pool.wait_ge(const_step, 3)
            pool.affine_select(out=diag[:, :], in_=diag[:, :], compare_op=ALU.not_equal, fill=1.0, base=SIDE + KC - 1,
                               pattern=[[-1, NCAT + KC - 1]], channel_multiplier=KC).then_inc(const_step, 1)
            pool.affine_select(out=own_batch[:, :], in_=own_batch[:, :], compare_op=ALU.is_ge, fill=0.0, base=0,
                               pattern=[[-R1, B]], channel_multiplier=1).then_inc(const_step, 1)
            pool.wait_ge(const_step, 6)
            pool.affine_select(out=own_batch[:, :], in_=own_batch[:, :], compare_op=ALU.is_ge, fill=0.0, base=R1 - 1,
                               pattern=[[R1, B]], channel_multiplier=-1).then_inc(const_step, 1)
            pool.iota(expert_no[:, :], pattern=[[1, E]], base=0, channel_multiplier=0,
                      allow_small_or_imprecise_dtypes=True).then_inc(const_step, 1)
            pool.memset(u0[:, :, R0:U0], 1.0).then_inc(const_step, 1)

            def split_exp_b(loaded, dst, src):
                pool.wait_ge(loaded, 16)
                pool.tensor_copy(dst[:, :, :].rearrange("p c (e r) -> p c e r", e=E),
                                 src[:, :, :].rearrange("p e (c r) -> p c e r", c=KC)).then_inc(exp_b_split, 1)

            split_exp_b(exp_b0_in, exp_b0_c, exp_b0_n)
            pool.wait_ge(lora_b0_in, 32)
            pool.tensor_copy(lora_b0_n[:, :, R0:U0], bias0_n[:, :].unsqueeze(2)).then_inc(bias_placed, 1)
            pool.wait_ge(*high_of(F_M0_G0))
            pool.tensor_copy(m0[1][:, :, 0:SIDE], m0[0][:, :, 0:SIDE]).then_inc(m0_copied, 1)

            split_exp_b(exp_b1_in, exp_b1_c, exp_b1_n)

            def place_a0(t, side):
                pool.tensor_copy(m0[side][:, :, SIDE:N0], lora_a0_g[:, bass.ds(t, 1), :, :].rearrange("p a c r -> p (a c) r")
                                 ).then_inc(a0_placed, 1)

            def place_a1(t, side):
                at = A1_AT[side]
                src = lora_a1_g[:, bass.ds(t, 1), :, :].rearrange("p a c r -> p (a c) r")
                pool.tensor_copy(m1_b[HIGH][:, :, at:at + R1], src).then_inc(a1_high, 1)
                pool.wait_ge(a1_high, t + 1)
                pool.tensor_tensor(m1_b[LOW][:, :, at:at + R1], src,
                                   m1_b[HIGH][:, :, at:at + R1].bitcast(F32), ALU.subtract).then_inc(a1_placed, 1)

            pool.wait_ge(a0_gathered, 16 * B)
            place_a0(0, 0)
            place_a0(1, 1)
            pool.wait_ge(a1_gathered, 16 * B)
            for c in range(KC):
                pool.wait_ge(*high_of(F_M1[c] + 1))
                pool.tensor_tensor(m1_b[LOW][:, c, R1:R1 + NB], m1_f[:, c % 2, 0:NB],
                                   m1_b[HIGH][:, c, R1:R1 + NB].bitcast(F32), ALU.subtract).then_inc(m1_low, 1)
                pool.tensor_tensor(m1_a[LOW][:, c, :], m1_f[:, c % 2, NB:NCAT],
                                   m1_a[HIGH][:, c, :].bitcast(F32), ALU.subtract).then_inc(m1_low, 1)
            place_a1(0, 0)
            place_a1(1, 1)
            for p in range(1, PAIRS):
                for side in range(2):
                    t = 2 * p + side
                    pool.wait_ge(l0_scored, t - 1)
                    place_a0(t, side)
                for side in range(2):
                    t = 2 * p + side
                    pool.wait_ge(side_scored, t - 1)
                    place_a1(t, side)

        @block.tensor
        def _(pe):
            def turn(dst, src, k=P, start=True):
                return pe.matmul(dst, src, ident[0:k, 0:k], start=start, stop=True, is_transpose=True,
                                 skip_group_check=True)

            def products(dst, left, right, start, stop):
                for n, (a, b) in enumerate(PASSES):
                    last = pe.matmul(dst, left[a], right[b], start=start and n == 0, stop=stop and n == 2,
                                     skip_group_check=True)
                return last

            def fill(n):
                if n >= 8:
                    pe.wait_ge(*emptied(n - 8))
                return banks[n % 8]

            pe.wait_ge(const_step, 4)
            pe.wait_ge(exp_a0_in, 32)
            bank = fill(F_A0)
            for k in range(KC):
                last = turn(bank[:, k * P:(k + 1) * P], exp_a0_n[:, k:D:KC])
            last.then_inc(prep_filled, 1)
            bank = fill(F_ROUTE0)
            for k in range(KC):
                last = turn(bank[:, k * E:(k + 1) * E], route0_n[:, k:D:KC], E)
            last.then_inc(prep_filled, 1)
            pe.wait_ge(exp_b_split, 1)
            bank = fill(F_B0)
            for c in range(KC):
                last = turn(bank[:, c * P:(c + 1) * P], exp_b0_c[:, c, :])
            last.then_inc(prep_filled, 1)
            pe.wait_ge(*emptied(F_A0))
            pe.wait_ge(*emptied(F_ROUTE0))
            pe.wait_ge(w0_in, 16)
            for n, chunks in ((F_M0, range(KC - 1)), (F_M0_G0, range(KC - 1, KC))):
                bank = fill(n)
                for c in chunks:
                    at = (c - chunks[0]) * SIDE
                    for k in range(KC):
                        last = pe.matmul(bank[:, at:at + SIDE], w0_n[:, k, c:D:KC], cat0_t[:, k, :],
                                         start=k == 0, stop=k == KC - 1, skip_group_check=True)
                if n == F_M0_G0:
                    pe.wait_ge(bias_placed, 1)
                    for k in range(KC):
                        last = pe.matmul(bank[0:U0, SIDE:2 * SIDE], lora_b0_n[:, k, :], cat0_t[:, k, :],
                                         start=k == 0, stop=k == KC - 1, skip_group_check=True)
                last.then_inc(prep_filled, 1)
            pe.wait_ge(b1_gathered, 16 * B)
            bank = fill(F_LORA_B1)
            for k in range(KC):
                last = turn(bank[:, k * P:(k + 1) * P], lora_b1_g[:, k * P:(k + 1) * P])
            last.then_inc(prep_filled, 1)
            pe.wait_ge(exp_a1_in, 32)
            bank = fill(F_A1)
            for k in range(KC):
                last = turn(bank[:, k * P:(k + 1) * P], exp_a1_n[:, k * P:(k + 1) * P])
            last.then_inc(prep_filled, 1)
            bank = fill(F_ROUTE1)
            for k in range(KC):
                last = turn(bank[:, k * E:(k + 1) * E], route1_n[:, k * P:(k + 1) * P], E)
            last.then_inc(prep_filled, 1)
            pe.wait_ge(w_base_in, 16)
            for j in range(KC):
                bank = fill(F_BASE + j)
                for k in range(KC):
                    last = turn(bank[:, k * P:(k + 1) * P], w_base_n[:, j, k * P:(k + 1) * P])
                last.then_inc(prep_filled, 1)
            pe.wait_ge(*emptied(F_BASE + KC - 1))
            for n, (a, b) in enumerate(BLOCKS):
                bank = fill(F_G1 + n)
                for k in range(KC):
                    last = products(bank[:, 0:b - a], [t[:, k, :] for t in lora_b1_t], [t[:, k, a:b] for t in cat1_t],
                                    k == 0, k == KC - 1)
                last.then_inc(prep_filled, 1)
            pe.wait_ge(exp_b_split, 2)
            bank = fill(F_B1)
            for c in range(KC):
                last = turn(bank[:, c * P:(c + 1) * P], exp_b1_c[:, c, :])
            last.then_inc(prep_filled, 1)
            pe.wait_ge(w1_in, 16)

            def turn_w1(c):
                bank = fill(F_W1[c])
                for k in range(KC):
                    last = turn(bank[:, k * P:(k + 1) * P], w1_n[:, c, k * P:(k + 1) * P])
                last.then_inc(prep_filled, 1)

            turn_w1(0)
            for c in range(KC):
                if c + 1 < KC:
                    turn_w1(c + 1)
                pe.wait_ge(*emptied(F_W1[c]))
                for n, (a, b) in enumerate(BLOCKS):
                    bank = fill(F_M1[c] + n)
                    for k in range(KC):
                        last = products(bank[:, 0:b - a], [t[:, c % 2, k, :] for t in w1_t],
                                        [t[:, k, a:b] for t in cat1_t], k == 0, k == KC - 1)
                    last.then_inc(prep_filled, 1)
            pe.wait_ge(*high_of(FILLS - 1))
            pe.wait_ge(*low_of(FILLS - 1))

            def turn_x(q, side):
                if side == 0:
                    pe.wait_ge(x_loaded, 16 * (q + 1))
                    if q > 0:
                        pe.wait_ge(x1_summed, 2 * q)
                else:
                    pe.wait_ge(xt_copied, 2 * q + side)
                for c in range(KC):
                    last = turn(bank_x[:, c * P:(c + 1) * P], x_in[:, side, c:D:KC])
                last.then_inc(xt_filled, 1)

            def score0(q, side):
                t = 2 * q + side
                pe.wait_ge(xt_copied, t + 1)
                pe.wait_ge(a0_placed, t + 1)
                if q > 0:
                    pe.wait_ge(x1_summed if side == 0 else gated0t_low, 2 * q)
                for c in range(KC):
                    last = pe.matmul(bank_l0[side][:, 0:N0], x_t[:, c, side, :], m0[side][:, c, :],
                                     start=c == 0, stop=c == KC - 1, skip_group_check=True)
                last.then_inc(l0_scored, 1)

            def turn_u0(q, side):
                pe.wait_ge(u0_copied, 2 * q + side + 1)
                turn(bank_l0[side][0:U0, U0_T:U0_T + P], u0[:, side, :], start=False).then_inc(u0t_filled, 1)

            def adapt0(q, side):
                pe.wait_ge(u0t_copied, 2 * q + side + 1)
                pe.matmul(bank_l0[side][:, 0:SIDE], u0_t[:, side, :], g0[:, :], start=False, stop=True,
                          skip_group_check=True).then_inc(l0_ready, 1)

            def turn_gated0(q, side):
                pe.wait_ge(gated0_ready, 2 * q + side + 1)
                turn(bank_l0[side][:, GATED0_T:GATED0_T + P], gated0[:, side, :], start=False
                     ).then_inc(gated0t_filled, 1)

            def ffn0(q):
                pe.wait_ge(gated0t_low, 2 * q + 2)
                for r, bank in enumerate((bank_x, bank_l0[0])):
                    for j in range(2):
                        c = 2 * r + j
                        last = products(bank[:, j * 2 * P:(j + 1) * 2 * P], [w[:, c, :] for w in exp_b0_t],
                                        [g[:, :, :] for g in gated0_t], True, True)
                    last.then_inc(x1_filled, 1)

            def side1(p, side):
                t = 2 * p + side
                pe.wait_ge(x1_low, 2 * p + 2)
                pe.wait_ge(a1_placed, t + 1)
                if p > 0:
                    pe.wait_ge(y_ready, t - 1)
                a = 0 if side == 0 else R1
                for c in range(KC):
                    last = products(b_bank(side, 0, R1 + NB), [v[:, c, side, :] for v in x1_t],
                                    [m[:, c, a:a + R1 + NB] for m in m1_b], c == 0, c == KC - 1)
                last.then_inc(side_scored, 1)

            def base1(p, side):
                for c in range(KC):
                    last = products(acc[side][:, 512:512 + HB], [v[:, c, side, :] for v in x1_t],
                                    [m[:, c, :] for m in m1_a], c == 0, False)
                last.then_inc(base_scored, 1)

            def turn_u1(p, side):
                t = 2 * p + side
                pe.wait_ge(u1_copied, t + 1)
                if p > 0 or side > 0:
                    pe.wait_ge(gated1t_low, t)
                turn(bank_small[:, side * P:(side + 1) * P], u1[:, side, :, :]).then_inc(u1t_filled, 1)

            def adapt1(p, side):
                pe.wait_ge(u1t_low, 2 * p + side + 1)
                left = [u[:, side, :] for u in u1_t]
                at = SIDE_AT[side]
                products(b_bank(side, at, at + NB), left, [g[:, 0:NB] for g in g1], False, False)
                products(acc[side][:, 512:512 + HB], left, [g[:, NB:NCAT] for g in g1], False, False
                         ).then_inc(l1_ready, 1)

            def turn_gated1(p, side):
                t = 2 * p + side
                pe.wait_ge(gated1_ready, t + 1)
                turn(bank_small[:, (2 + side) * P:(3 + side) * P], gated1[:, side, :]).then_inc(gated1t_filled, 1)

            def ffn1(p, side):
                pe.wait_ge(gated1t_low, 2 * p + side + 1)
                left = [g[:, side, :] for g in gated1_t]
                at = SIDE_AT[side] + SIDE
                wide = [e[:, :, :].rearrange("p a c -> p (a c)") for e in exp_b1_t]
                products(b_bank(side, at, at + HB), left, [w[:, 0:HB] for w in wide], False, True)
                products(acc[side][:, 512:512 + HB], left, [w[:, HB:D] for w in wide], False, True
                         ).then_inc(y_filled, 1)

            pe.wait_ge(m0_copied, 1)
            turn_x(0, 0)
            turn_x(0, 1)
            score0(0, 0)
            score0(0, 1)
            turn_u0(0, 0)
            turn_u0(0, 1)
            adapt0(0, 0)
            adapt0(0, 1)
            turn_gated0(0, 0)
            turn_gated0(0, 1)
            ffn0(0)
            pe.wait_ge(m1_low, 2 * KC)
            for p in range(PAIRS):
                q = p + 1
                more = q < PAIRS
                side1(p, 0)
                if more:
                    turn_x(q, 0)
                base1(p, 0)
                if more:
                    turn_x(q, 1)
                turn_u1(p, 0)
                if more:
                    score0(q, 0)
                adapt1(p, 0)
                if more:
                    score0(q, 1)
                side1(p, 1)
                if more:
                    turn_u0(q, 0)
                    turn_u0(q, 1)
                turn_gated1(p, 0)
                if more:
                    adapt0(q, 0)
                    adapt0(q, 1)
                base1(p, 1)
                turn_u1(p, 1)
                if more:
                    turn_gated0(q, 0)
                ffn1(p, 0)
                if more:
                    turn_gated0(q, 1)
                    ffn0(q)
                adapt1(p, 1)
                turn_gated1(p, 1)
                ffn1(p, 1)

        @block.scalar
        def _(act):
            def blocks(n, count, w):
                return banks[n % 8][:, 0:count * w].rearrange("p (k w) -> p k w", k=count)

            def copy(dst, src, **more):
                return act.activation(dst, src, ACT.Copy, **more)

            def filled(n):
                act.wait_ge(prep_filled, n + 1)

            filled(F_A0)
            copy(cat0_t[:, :, 0:ER], blocks(F_A0, KC, P)).then_inc(prep_high, 1)
            filled(F_B0)
            copy(exp_b0_t[HIGH][:, :, :], blocks(F_B0, KC, P)).then_inc(prep_high, 1)
            filled(F_M0)
            copy(m0[0][:, 0:KC - 1, 0:SIDE], blocks(F_M0, KC - 1, SIDE)).then_inc(prep_high, 1)
            filled(F_M0_G0)
            copy(m0[0][:, KC - 1, 0:SIDE], banks[F_M0_G0][:, 0:SIDE])
            copy(g0[:, :], banks[F_M0_G0][0:U0, SIDE:2 * SIDE]).then_inc(prep_high, 1)
            filled(F_LORA_B1)
            copy(lora_b1_t[HIGH][:, :, :], blocks(F_LORA_B1, KC, P)).then_inc(prep_high, 1)
            filled(F_A1)
            copy(cat1_t[HIGH][:, :, 0:ER], blocks(F_A1, KC, P)).then_inc(prep_high, 1)
            filled(F_ROUTE1)
            copy(cat1_t[HIGH][:, :, ER:SIDE], blocks(F_ROUTE1, KC, E)).then_inc(prep_high, 1)
            for j in range(KC):
                filled(F_BASE + j)
                copy(cat1_t[HIGH][:, :, SIDE + j * P:SIDE + (j + 1) * P], blocks(F_BASE + j, KC, P)).then_inc(prep_high, 1)
            for n, (a, b) in enumerate(BLOCKS):
                filled(F_G1 + n)
                copy(g1[HIGH][:, a:b], banks[(F_G1 + n) % 8][:, 0:b - a]).then_inc(prep_high, 1)
            filled(F_B1)
            copy(exp_b1_t[HIGH][:, :, :].rearrange("p a c -> p c a"), blocks(F_B1, KC, P), scale=SCALE_FFN1
                 ).then_inc(prep_high, 1)

            def high_w1(c):
                filled(F_W1[c])
                copy(w1_t[HIGH][:, c % 2, :, :], blocks(F_W1[c], KC, P)).then_inc(prep_high, 1)

            high_w1(0)
            for c in range(KC):
                if c + 1 < KC:
                    high_w1(c + 1)
                act.wait_ge(*low_of(F_M1[c]))
                copy(m1_b[HIGH][:, c, R1:R1 + NB], m1_f[:, c % 2, 0:NB]).then_inc(prep_high, 1)
                act.wait_ge(*low_of(F_M1[c] + 1))
                copy(m1_a[HIGH][:, c, :], m1_f[:, c % 2, NB:NCAT]).then_inc(prep_high, 1)

            def copy_xt(q, side):
                act.wait_ge(xt_filled, 2 * q + side + 1)
                copy(x_t[:, :, side, :], bank_x[:, :].rearrange("p (c t) -> p c t", c=KC)).then_inc(xt_copied, 1)

            def copy_u0(q, side):
                act.wait_ge(l0_scored, 2 * q + side + 1)
                copy(u0[:, side, 0:R0], bank_l0[side][:, SIDE:N0], scale=SCALE0).then_inc(u0_copied, 1)

            def copy_u0t(q, side):
                act.wait_ge(u0t_filled, 2 * q + side + 1)
                copy(u0_t[:, side, :], bank_l0[side][0:U0, U0_T:U0_T + P]).then_inc(u0t_copied, 1)

            def high_gated0(q, side):
                act.wait_ge(gated0t_filled, 2 * q + side + 1)
                copy(gated0_t[HIGH][:, side, :], bank_l0[side][:, GATED0_T:GATED0_T + P]).then_inc(gated0t_high, 1)

            def high_x1(q, r):
                act.wait_ge(x1_summed, 2 * q + r + 1)
                if r == 0 and q > 0:
                    act.wait_ge(base_scored, 2 * q)
                copy(x1_t[HIGH][:, 2 * r:2 * r + 2, :, :], x1_f[:, 2 * r:2 * r + 2, :, :]).then_inc(x1_high, 1)

            def copy_u1(p, side):
                act.wait_ge(side_scored, 2 * p + side + 1)
                at = U1_AT[side]
                copy(u1[:, side, :, :], acc[side][:, at:at + R1].unsqueeze(1).to_broadcast([P, B, R1])
                     ).then_inc(u1_copied, 1)

            def high_u1(p, side):
                t = 2 * p + side
                act.wait_ge(u1t_filled, t + 1)
                copy(u1_t[HIGH][:, side, :], bank_small[:, side * P:(side + 1) * P],
                     scale=own_batch[:, bass.ds(t, 1)]).then_inc(u1t_high, 1)

            def exp1(p, side):
                act.wait_ge(below_ready, 2 * p + side + 1)
                act.activation(expo[:, side, :], below[:, side, :], ACT.Exp).then_inc(expo_ready, 1)

            def high_gated1(p, side):
                act.wait_ge(gated1t_filled, 2 * p + side + 1)
                copy(gated1_t[HIGH][:, side, :], bank_small[:, (2 + side) * P:(3 + side) * P]).then_inc(gated1t_high, 1)

            copy_xt(0, 0)
            copy_xt(0, 1)
            copy_u0(0, 0)
            copy_u0(0, 1)
            copy_u0t(0, 0)
            copy_u0t(0, 1)
            high_gated0(0, 0)
            high_gated0(0, 1)
            high_x1(0, 0)
            high_x1(0, 1)
            for p in range(PAIRS):
                q = p + 1
                more = q < PAIRS
                copy_u1(p, 0)
                if more:
                    copy_xt(q, 0)
                    copy_xt(q, 1)
                high_u1(p, 0)
                if more:
                    copy_u0(q, 0)
                exp1(p, 0)
                if more:
                    copy_u0(q, 1)
                copy_u1(p, 1)
                if more:
                    copy_u0t(q, 0)
                    copy_u0t(q, 1)
                high_gated1(p, 0)
                high_u1(p, 1)
                if more:
                    high_gated0(q, 0)
                    high_gated0(q, 1)
                    high_x1(q, 0)
                    high_x1(q, 1)
                exp1(p, 1)
                high_gated1(p, 1)

        @block.vector
        def _(dve):
            def blocks(n, count, w):
                return banks[n % 8][:, 0:count * w].rearrange("p (k w) -> p k w", k=count)

            def low(dst, exact, high):
                return dve.tensor_tensor(dst, exact, high.bitcast(F32), ALU.subtract)

            steps = [0]

            def finished(ins):
                steps[0] += 1
                ins.then_inc(dve_step, 1)
                dve.wait_ge(dve_step, steps[0])

            dve.wait_ge(prep_filled, F_ROUTE0 + 1)
            dve.tensor_copy(cat0_t[:, :, ER:SIDE], blocks(F_ROUTE0, KC, E)).then_inc(prep_low, 1)
            dve.wait_ge(*high_of(F_B0))
            low(exp_b0_t[LOW][:, :, :], blocks(F_B0, KC, P), exp_b0_t[HIGH][:, :, :]).then_inc(prep_low, 1)
            dve.wait_ge(*high_of(F_LORA_B1))
            low(lora_b1_t[LOW][:, :, :], blocks(F_LORA_B1, KC, P), lora_b1_t[HIGH][:, :, :]).then_inc(prep_low, 1)
            dve.wait_ge(*high_of(F_A1))
            low(cat1_t[LOW][:, :, 0:ER], blocks(F_A1, KC, P), cat1_t[HIGH][:, :, 0:ER]).then_inc(prep_low, 1)
            dve.wait_ge(*high_of(F_ROUTE1))
            low(cat1_t[LOW][:, :, ER:SIDE], blocks(F_ROUTE1, KC, E), cat1_t[HIGH][:, :, ER:SIDE]).then_inc(prep_low, 1)
            for j in range(KC):
                a, b = SIDE + j * P, SIDE + (j + 1) * P
                dve.wait_ge(*high_of(F_BASE + j))
                low(cat1_t[LOW][:, :, a:b], blocks(F_BASE + j, KC, P), cat1_t[HIGH][:, :, a:b]).then_inc(prep_low, 1)
            for n, (a, b) in enumerate(BLOCKS):
                dve.wait_ge(*high_of(F_G1 + n))
                low(g1[LOW][:, a:b], banks[(F_G1 + n) % 8][:, 0:b - a], g1[HIGH][:, a:b]).then_inc(prep_low, 1)
            dve.wait_ge(*high_of(F_B1))
            dve.scalar_tensor_tensor(out=exp_b1_t[LOW][:, :, :].rearrange("p a c -> p c a"), in0=blocks(F_B1, KC, P),
                                     scalar=SCALE_FFN1,
                                     in1=exp_b1_t[HIGH][:, :, :].bitcast(F32).rearrange("p a c -> p c a"),
                                     op0=ALU.mult, op1=ALU.subtract).then_inc(prep_low, 1)

            def low_w1(c):
                dve.wait_ge(*high_of(F_W1[c]))
                low(w1_t[LOW][:, c % 2, :, :], blocks(F_W1[c], KC, P), w1_t[HIGH][:, c % 2, :, :]).then_inc(prep_low, 1)

            dve.wait_ge(const_step, 9)
            low_w1(0)
            for c in range(KC):
                if c + 1 < KC:
                    low_w1(c + 1)
                if c >= 2:
                    dve.wait_ge(*high_of(F_M1[c - 2] + 1))
                    dve.wait_ge(m1_low, 2 * (c - 1))
                for n, (a, b) in enumerate(BLOCKS):
                    dve.wait_ge(prep_filled, F_M1[c] + n + 1)
                    at = KC - 1 - c
                    dve.tensor_tensor(m1_f[:, c % 2, a:b], banks[(F_M1[c] + n) % 8][:, 0:b - a],
                                      diag[:, at + a:at + b], ALU.add).then_inc(prep_low, 1)

            def route0(q, side):
                t = 2 * q + side
                scores = bank_l0[side][:, ER:SIDE]
                dve.wait_ge(l0_ready, t + 1)
                finished(dve.max(top0[:, side, :], scores))
                finished(dve.max_index(top0_at[:, side, :], top0[:, side, :], scores))
                finished(dve.scalar_tensor_tensor(out=gate0[:, side, :], in0=expert_no[:, :], scalar=top0_at[:, side, 0:1],
                                                  in1=scores, op0=ALU.is_equal, op1=ALU.mult))
                dve.tensor_tensor(gated0[:, side, :].rearrange("p (e r) -> p e r", e=E),
                                  bank_l0[side][:, 0:ER].rearrange("p (e r) -> p e r", e=E),
                                  gate0[:, side, :].unsqueeze(2).to_broadcast([P, E, RE]), ALU.mult
                                  ).then_inc(gated0_ready, 1)

            def low_gated0(q, side):
                dve.wait_ge(gated0t_high, 2 * q + side + 1)
                low(gated0_t[LOW][:, side, :], bank_l0[side][:, GATED0_T:GATED0_T + P], gated0_t[HIGH][:, side, :]
                    ).then_inc(gated0t_low, 1)

            def sum_x1(q, r):
                dve.wait_ge(x1_filled, 2 * q + r + 1)
                dve.tensor_tensor(x1_f[:, 2 * r:2 * r + 2, :, :],
                                  (bank_x, bank_l0[0])[r][:, :].rearrange("p (c s t) -> p c s t", c=2, s=2),
                                  x_t[:, 2 * r:2 * r + 2, :, :], ALU.add).then_inc(x1_summed, 1)

            def low_x1(q, r):
                dve.wait_ge(x1_high, 2 * q + r + 1)
                low(x1_t[LOW][:, 2 * r:2 * r + 2, :, :], x1_f[:, 2 * r:2 * r + 2, :, :],
                    x1_t[HIGH][:, 2 * r:2 * r + 2, :, :]).then_inc(x1_low, 1)

            def low_u1(p, side):
                t = 2 * p + side
                dve.wait_ge(u1t_high, t + 1)
                dve.scalar_tensor_tensor(out=u1_t[LOW][:, side, :], in0=bank_small[:, side * P:(side + 1) * P],
                                         scalar=own_batch[:, bass.ds(t, 1)], in1=u1_t[HIGH][:, side, :].bitcast(F32),
                                         op0=ALU.mult, op1=ALU.subtract).then_inc(u1t_low, 1)

            def route1(p, side):
                t = 2 * p + side
                at = SIDE_AT[side]
                scores = acc[side][:, at + ER:at + SIDE]
                dve.wait_ge(l1_ready, t + 1)
                finished(dve.max(top1[:, side, :], scores))
                dve.tensor_scalar(below[:, side, :], scores, top1[:, side, 0:1], None, ALU.subtract).then_inc(below_ready, 1)
                finished(dve.max_index(top1_at[:, side, :], top1[:, side, :], scores))
                finished(dve.tensor_scalar(first[:, side, :], expert_no[:, :], top1_at[:, side, 0:1], None, ALU.is_equal))
                finished(dve.scalar_tensor_tensor(out=chosen[:, side, :], in0=expert_no[:, :], scalar=top1_at[:, side, 1:2],
                                                  in1=first[:, side, :], op0=ALU.is_equal, op1=ALU.add))
                dve.wait_ge(expo_ready, t + 1)
                finished(dve.scalar_tensor_tensor(out=weight[:, side, :], in0=chosen[:, side, :], scalar=1.0,
                                                  in1=expo[:, side, :], op0=ALU.mult, op1=ALU.mult,
                                                  accum_out=total[:, side:side + 1]))
                finished(dve.reciprocal(inverse[:, side:side + 1], total[:, side:side + 1]))
                dve.scalar_tensor_tensor(out=gated1[:, side, :].rearrange("p (e r) -> p e r", e=E),
                                         in0=acc[side][:, at:at + ER].rearrange("p (e r) -> p e r", e=E),
                                         scalar=inverse[:, side:side + 1],
                                         in1=weight[:, side, :].unsqueeze(2).to_broadcast([P, E, RE]),
                                         op0=ALU.mult, op1=ALU.mult).then_inc(gated1_ready, 1)

            def low_gated1(p, side):
                dve.wait_ge(gated1t_high, 2 * p + side + 1)
                low(gated1_t[LOW][:, side, :], bank_small[:, (2 + side) * P:(3 + side) * P], gated1_t[HIGH][:, side, :]
                    ).then_inc(gated1t_low, 1)

            def sum_y(p, side):
                t = 2 * p + side
                dve.wait_ge(y_filled, t + 1)
                if p > 0:
                    dve.wait_ge(stored[side], 16 * p)
                dve.tensor_tensor(y[:, side, :].rearrange("p (a b) -> p a b", a=2), base_part(side),
                                  b_base_all[:, :].rearrange("p (a b) -> p a b", a=2), ALU.add).then_inc(y_ready, 1)

            route0(0, 0)
            route0(0, 1)
            low_gated0(0, 0)
            low_gated0(0, 1)
            sum_x1(0, 0)
            sum_x1(0, 1)
            low_x1(0, 0)
            low_x1(0, 1)
            dve.wait_ge(b_base_in, 16)
            for p in range(PAIRS):
                q = p + 1
                more = q < PAIRS
                low_u1(p, 0)
                route1(p, 0)
                low_gated1(p, 0)
                if more:
                    route0(q, 0)
                    route0(q, 1)
                low_u1(p, 1)
                if more:
                    low_gated0(q, 0)
                sum_y(p, 0)
                if more:
                    low_gated0(q, 1)
                    sum_x1(q, 0)
                    sum_x1(q, 1)
                    low_x1(q, 0)
                    low_x1(q, 1)
                route1(p, 1)
                low_gated1(p, 1)
                sum_y(p, 1)


_INS = ["x", "itok_B_0_4", "itok_B_0_15", "L0_cond_weight", "L0_cond_bias", "L0_cond_lora_A", "L0_cond_lora_B",
        "L0_ffn_route_w", "L0_ffn_A", "L0_ffn_Bw", "L1_cond_W", "L1_cond_lora_A", "L1_cond_lora_B", "L1_ffn_W_base",
        "L1_ffn_b_base", "L1_ffn_W_router", "L1_ffn_A_stack", "L1_ffn_B_stack"]


def kernel(**inputs):
    import numpy as _np
    import concourse.bacc as _bacc
    from concourse import mybir as _mybir
    from concourse.bass_utils import run_bass_kernel_spmd as _run

    nc = _bacc.Bacc("TRN2", target_bir_lowering=False, num_devices=1)
    arrays, args = {}, []
    for name in _INS:
        a = _np.ascontiguousarray(inputs[name])
        arrays[f"in_{name}_dram"] = a
        args.append(nc.dram_tensor(f"in_{name}_dram", a.shape, _mybir.dt.from_np(a.dtype), kind="ExternalInput").ap())
    out = nc.dram_tensor("out_0_dram", inputs["x"].shape, _mybir.dt.float32, kind="ExternalOutput").ap()
    adaln_ffn_kernel(nc, *args, out)
    r = _run(nc, [arrays], core_ids=[0])
    return r.results[0]["out_0_dram"]
```

```python
from contextlib import ExitStack

import concourse.bass as bass
from concourse import mybir

F32 = mybir.dt.float32
F32R = mybir.dt.float32r
I32 = mybir.dt.int32
U32 = mybir.dt.uint32
ALU = mybir.AluOpType
ACT = mybir.ActivationFunctionType

P = 128
HIGH, LOW = 0, 1
PASSES = ((HIGH, HIGH), (HIGH, LOW), (LOW, HIGH))


def adaln_ffn_kernel(nc, x, label0, label1, w0, bias0, lora_a0, lora_b0, route0, exp_a0, exp_b0,
                     w1, lora_a1, lora_b1, w_base, b_base, route1, exp_a1, exp_b1, out):
    B, S, D = x.shape
    L0, _, R0 = lora_a0.shape
    L1, _, R1 = lora_a1.shape
    E, RE, _ = exp_a0.shape
    KC = D // P
    ER = E * RE
    SIDE = ER + E
    N0 = SIDE + R0
    U0 = R0 + 1
    HB = D // 2
    NB = SIDE + HB
    NCAT = SIDE + D
    WB = R1 + NB + R1
    BR = B * R1
    BLOCKS = ((0, NB), (NB, NCAT))
    PAIRS = B // 2
    SCALE0 = 16 / 32
    SCALE_FFN1 = 32.0 / 16
    assert S == P and ER == P and BR == P and D % P == 0 and R1 == RE

    with ExitStack() as ctx:
        def sb(name, shape, dt=F32):
            return ctx.enter_context(nc.sbuf_tensor(name, shape, dt))

        def sem(name):
            return ctx.enter_context(nc.semaphore(name))

        ident = sb("ident", [P, P])
        diag = sb("diag", [P, NCAT + KC - 1])
        own_batch = sb("own_batch", [P, B])
        expert_no = sb("expert_no", [P, E])
        exp_a0_n = sb("exp_a0_n", [ER, D])
        route0_n = sb("route0_n", [E, D])
        w0_n = sb("w0_n", [P, KC, D])
        lora_b0_n = sb("lora_b0_n", [P, KC, U0])
        bias0_n = sb("bias0_n", [P, KC])
        exp_b0_n = sb("exp_b0_n", [P, E, KC * RE])
        w_base_n = sb("w_base_n", [P, KC, D])
        exp_a1_n = sb("exp_a1_n", [ER, D])
        route1_n = sb("route1_n", [E, D])
        w1_n = sb("w1_n", [P, KC, D])
        exp_b1_n = sb("exp_b1_n", [P, E, KC * RE])
        b_base_all = sb("b_base_all", [P, D])
        labels = sb("labels", [1, 2, B], I32)
        lora_a0_g = sb("lora_a0_g", [P, B, KC, R0])
        lora_a1_g = sb("lora_a1_g", [P, B, KC, R1])
        lora_b1_g = sb("lora_b1_g", [BR, D])
        exp_b0_c = sb("exp_b0_c", [P, KC, ER])
        exp_b1_c = sb("exp_b1_c", [P, KC, ER])
        cat0_t = sb("cat0_t", [P, KC, SIDE])
        m0 = [sb(f"m0_{s}", [P, KC, N0]) for s in range(2)]
        g0 = sb("g0", [U0, SIDE])
        exp_b0_t = [sb(f"exp_b0_t{h}", [ER, KC, P], F32R) for h in range(2)]
        lora_b1_t = [sb(f"lora_b1_t{h}", [P, KC, BR], F32R) for h in range(2)]
        cat1_t = [sb(f"cat1_t{h}", [P, KC, NCAT], F32R) for h in range(2)]
        w1_t = [sb(f"w1_t{h}", [P, 2, KC, P], F32R) for h in range(2)]
        g1 = [sb(f"g1_{h}", [BR, NCAT], F32R) for h in range(2)]
        m1_f = sb("m1_f", [P, 2, NCAT])
        m1_b = [sb(f"m1_b{h}", [P, KC, WB], F32R) for h in range(2)]
        m1_a = [sb(f"m1_a{h}", [P, KC, HB], F32R) for h in range(2)]
        exp_b1_t = [sb(f"exp_b1_t{h}", [ER, P, KC], F32R) for h in range(2)]
        x_in = sb("x_in", [P, 2, D])
        x_t = [sb(f"x_t{i}", [P, KC, 2, P]) for i in range(2)]
        x1_f = sb("x1_f", [P, KC, 2, P])
        x1_t = [[sb(f"x1_t{i}_{h}", [P, KC, 2, P], F32R) for h in range(2)] for i in range(2)]
        u0 = sb("u0", [P, 2, U0])
        u0_t = sb("u0_t", [U0, 2, P])
        top0 = sb("top0", [P, 2, 8])
        top0_at = sb("top0_at", [P, 2, 8], U32)
        gate0 = sb("gate0", [P, 2, E])
        gated0 = sb("gated0", [P, 2, ER])
        gated0_t = [sb(f"gated0_t{h}", [ER, 2, P], F32R) for h in range(2)]
        u1 = sb("u1", [P, 2, B, R1])
        u1_t = [sb(f"u1_t{h}", [BR, 2, P], F32R) for h in range(2)]
        top1 = sb("top1", [P, 2, 8])
        top1_at = sb("top1_at", [P, 2, 8], U32)
        below = sb("below", [P, 2, E])
        expo = sb("expo", [P, 2, E])
        first = sb("first", [P, 2, E])
        chosen = sb("chosen", [P, 2, E])
        weight = sb("weight", [P, 2, E])
        total = sb("total", [P, 2])
        inverse = sb("inverse", [P, 2])
        gated1 = sb("gated1", [P, 2, ER])
        gated1_t = [sb(f"gated1_t{h}", [ER, 2, P], F32R) for h in range(2)]
        y = sb("y", [P, 2, D])

        bank_x = ctx.enter_context(nc.psum_tensor("bank_x", [P, 512], F32))
        bank_l0 = [ctx.enter_context(nc.psum_tensor(f"bank_l0_{s}", [P, 512], F32)) for s in range(2)]
        bank_small = ctx.enter_context(nc.psum_tensor("bank_small", [P, 512], F32))
        acc = [ctx.enter_context(nc.psum_tensor(f"acc_{s}", [P, 1024], F32)) for s in range(2)]
        banks = [bank_x[:, :], bank_l0[0][:, :], bank_l0[1][:, :], bank_small[:, :],
                 acc[0][:, 0:512], acc[0][:, 512:1024], acc[1][:, 0:512], acc[1][:, 512:1024]]

        U0_T, GATED0_T = N0, N0 + P
        SIDE_AT = (R1, 0)
        U1_AT = (0, NB)
        A1_AT = (0, R1 + NB)

        def base_part(s):
            at = SIDE_AT[s] + SIDE
            w = 512 - at
            return acc[s][:, at:at + 2 * w].rearrange("p (a b) -> p a b", a=2)[:, :, 0:HB]

        labels_in, x_loaded, a0_gathered, b1_gathered, a1_gathered = (
            sem(n) for n in ("labels_in", "x_loaded", "a0_gathered", "b1_gathered", "a1_gathered"))
        exp_a0_in, lora_b0_in, exp_b0_in, exp_a1_in, exp_b1_in, b_base_in = (
            sem(n) for n in ("exp_a0_in", "lora_b0_in", "exp_b0_in", "exp_a1_in", "exp_b1_in", "b_base_in"))
        w0_in, w_base_in, w1_in = ([sem(f"{n}_in_{i}") for i in range(2)] for n in ("w0", "w_base", "w1"))
        const_step, exp_b_split, bias_placed, m0_copied, a0_placed, a1_high, a1_placed = (
            sem(n) for n in ("const_step", "exp_b_split", "bias_placed", "m0_copied", "a0_placed", "a1_high", "a1_placed"))
        stored = [sem(f"stored_{s}") for s in range(2)]
        prep_filled, prep_high, prep_low, m1_low = (sem(n) for n in ("prep_filled", "prep_high", "prep_low", "m1_low"))
        xt_filled, xt_copied, l0_scored, u0_copied, u0t_filled, u0t_copied, l0_ready = (
            sem(n) for n in ("xt_filled", "xt_copied", "l0_scored", "u0_copied", "u0t_filled", "u0t_copied", "l0_ready"))
        gated0_ready, gated0t_filled, gated0t_high, gated0t_low, x1_filled, x1_summed, x1_high, x1_low = (
            sem(n) for n in ("gated0_ready", "gated0t_filled", "gated0t_high", "gated0t_low", "x1_filled", "x1_summed",
                             "x1_high", "x1_low"))
        side_scored, base_scored, u1_copied, u1t_filled, u1t_high, u1t_low, l1_ready = (
            sem(n) for n in ("side_scored", "base_scored", "u1_copied", "u1t_filled", "u1t_high", "u1t_low", "l1_ready"))
        below_ready, expo_ready, gated1_ready, gated1t_filled, gated1t_high, gated1t_low, y_filled, y_ready, dve_step = (
            sem(n) for n in ("below_ready", "expo_ready", "gated1_ready", "gated1t_filled", "gated1t_high", "gated1t_low",
                             "y_filled", "y_ready", "dve_step"))

        F_A0, F_ROUTE0, F_A1, F_ROUTE1, F_M0, F_M0_G0, F_BASE = range(7)
        F_B0 = F_BASE + KC
        F_W1 = [F_B0 + 1, F_B0 + 2, F_B0 + 5, F_B0 + 8]
        F_M1 = [F_B0 + 3, F_B0 + 6, F_B0 + 9, F_B0 + 11]
        F_LORA_B1 = F_B0 + 13
        F_B1, F_G1 = F_LORA_B1 + 1, F_LORA_B1 + 2
        BANK_OF = (4, 5, 6, 7, 3, 1, 4, 5, 6, 7, 3, 4, 5, 6, 7, 3, 4, 5, 3, 6, 7, 4, 5, 3, 6, 7, 6)
        NOT_ON_ACT, NOT_ON_DVE = (F_ROUTE0,), (F_A0, F_M0, F_M0_G0)
        assert len(BANK_OF) == F_G1 + 2

        def high_of(n):
            return prep_high, sum(k not in NOT_ON_ACT for k in range(n + 1))

        def low_of(n):
            return prep_low, sum(k not in NOT_ON_DVE for k in range(n + 1))

        def emptied(n):
            return high_of(n) if n in NOT_ON_DVE else low_of(n)

        block = ctx.enter_context(nc.Block())

        @block.sync
        def _(sp):
            sp.dma_start(exp_a0_n[:, :], exp_a0.rearrange("e r d -> (e r) d")).then_inc(exp_a0_in, 16)
            sp.dma_start(route0_n[:, :], route0).then_inc(exp_a0_in, 16)
            w0_rows = w0.rearrange("(p k) i -> p k i", k=KC)
            for k in range(0, KC, 2):
                sp.dma_start(w0_n[:, k:k + 2, :], w0_rows[:, k:k + 2, :]).then_inc(w0_in[k // 2], 16)
            sp.dma_start(labels[0:1, 0, :], label0.rearrange("(a n) -> a n", a=1)).then_inc(labels_in, 16)
            sp.dma_start(labels[0:1, 1, :], label1.rearrange("(a n) -> a n", a=1)).then_inc(labels_in, 16)
            sp.dma_start(exp_a1_n[:, :], exp_a1.rearrange("e r d -> (e r) d")).then_inc(exp_a1_in, 16)
            sp.dma_start(route1_n[:, :], route1).then_inc(exp_a1_in, 16)
            sp.dma_start(bias0_n[:, :], bias0.rearrange("(p k) -> p k", k=KC)).then_inc(lora_b0_in, 16)
            sp.dma_start(lora_b0_n[:, :, 0:R0], lora_b0.rearrange("(p k) r -> p k r", k=KC)).then_inc(lora_b0_in, 16)
            base_rows = w_base.rearrange("(j p) o -> p j o", p=P)
            for j in range(0, KC, 2):
                sp.dma_start(w_base_n[:, j:j + 2, :], base_rows[:, j:j + 2, :]).then_inc(w_base_in[j // 2], 16)
            sp.dma_start(x_in[:, :, :], x[0:2].rearrange("b s d -> s b d")).then_inc(x_loaded, 16)
            sp.dma_start(exp_b0_n[:, :, :], exp_b0.rearrange("e (p c) r -> p e (c r)", c=KC)).then_inc(exp_b0_in, 16)
            w1_rows = w1.rearrange("(p c) o -> p c o", c=KC)
            for c in range(0, KC, 2):
                sp.dma_start(w1_n[:, c:c + 2, :], w1_rows[:, c:c + 2, :]).then_inc(w1_in[c // 2], 16)
            sp.wait_ge(labels_in, 32)
            _, named0 = nc.values_load_multi_w_load_instructions(
                labels[0:1, 0, :], engines=(mybir.EngineType.SP,), min_val=0, max_val=L0 - 1)
            _, named1 = nc.values_load_multi_w_load_instructions(
                labels[0:1, 1, :], engines=(mybir.EngineType.SP,), min_val=0, max_val=L1 - 1)
            for b in range(B):
                sp.dma_start(lora_a0_g[:, b:b + 1, :, :],
                             lora_a0[bass.ds(named0[b], 1)].rearrange("a (p c) r -> p a c r", c=KC)).then_inc(a0_gathered, 16)
            sp.dma_start(exp_b1_n[:, :, :], exp_b1.rearrange("e (p c) r -> p e (c r)", c=KC)).then_inc(exp_b1_in, 16)
            for b in range(B):
                sp.dma_start(lora_a1_g[:, b:b + 1, :, :],
                             lora_a1[bass.ds(named1[b], 1)].rearrange("a (p c) r -> p a c r", c=KC)).then_inc(a1_gathered, 16)
            for b in range(B):
                sp.dma_start(lora_b1_g[b * R1:(b + 1) * R1, :],
                             lora_b1[bass.ds(named1[b], 1)].rearrange("a r o -> (a r) o")).then_inc(b1_gathered, 16)
            sp.dma_start(b_base_all[:, :], b_base.rearrange("(a n) -> a n", a=1).to_broadcast([P, D])).then_inc(b_base_in, 16)

            def store(t, side):
                sp.wait_ge(y_ready, t + 1)
                sp.dma_start(out[bass.ds(t, 1)].rearrange("b s d -> (b s) d"), y[:, side, :]).then_inc(stored[side], 16)

            def load_x(q):
                sp.wait_ge(xt_filled, 2 * q)
                sp.dma_start(x_in[:, :, :], x[2 * q:2 * q + 2].rearrange("b s d -> s b d")).then_inc(x_loaded, 16)

            load_x(1)
            for p in range(PAIRS):
                if p + 2 < PAIRS:
                    load_x(p + 2)
                store(2 * p, 0)
                store(2 * p + 1, 1)
            for side in range(2):
                sp.wait_ge(stored[side], 16 * PAIRS)

        @block.gpsimd
        def _(pool):
            pool.memset(ident[:, :], 0.0).then_inc(const_step, 1)
            pool.memset(diag[:, :], 0.0).then_inc(const_step, 1)
            pool.memset(own_batch[:, :], 1.0).then_inc(const_step, 1)
            pool.wait_ge(const_step, 1)
            pool.affine_select(out=ident[:, :], in_=ident[:, :], compare_op=ALU.not_equal, fill=1.0, base=0,
                               pattern=[[-1, P]], channel_multiplier=1).then_inc(const_step, 1)
            pool.wait_ge(const_step, 3)
            pool.affine_select(out=diag[:, :], in_=diag[:, :], compare_op=ALU.not_equal, fill=1.0, base=SIDE + KC - 1,
                               pattern=[[-1, NCAT + KC - 1]], channel_multiplier=KC).then_inc(const_step, 1)
            pool.affine_select(out=own_batch[:, :], in_=own_batch[:, :], compare_op=ALU.is_ge, fill=0.0, base=0,
                               pattern=[[-R1, B]], channel_multiplier=1).then_inc(const_step, 1)
            pool.wait_ge(const_step, 6)
            pool.affine_select(out=own_batch[:, :], in_=own_batch[:, :], compare_op=ALU.is_ge, fill=0.0, base=R1 - 1,
                               pattern=[[R1, B]], channel_multiplier=-1).then_inc(const_step, 1)
            pool.iota(expert_no[:, :], pattern=[[1, E]], base=0, channel_multiplier=0,
                      allow_small_or_imprecise_dtypes=True).then_inc(const_step, 1)
            pool.memset(u0[:, :, R0:U0], 1.0).then_inc(const_step, 1)

            def split_exp_b(loaded, dst, src):
                pool.wait_ge(loaded, 16)
                pool.tensor_copy(dst[:, :, :].rearrange("p c (e r) -> p c e r", e=E),
                                 src[:, :, :].rearrange("p e (c r) -> p c e r", c=KC)).then_inc(exp_b_split, 1)

            pool.wait_ge(lora_b0_in, 32)
            pool.tensor_copy(lora_b0_n[:, :, R0:U0], bias0_n[:, :].unsqueeze(2)).then_inc(bias_placed, 1)

            def place_a0(t, side):
                pool.tensor_copy(m0[side][:, :, SIDE:N0], lora_a0_g[:, bass.ds(t, 1), :, :].rearrange("p a c r -> p (a c) r")
                                 ).then_inc(a0_placed, 1)

            def place_a1(t, side):
                at = A1_AT[side]
                src = lora_a1_g[:, bass.ds(t, 1), :, :].rearrange("p a c r -> p (a c) r")
                pool.tensor_copy(m1_b[HIGH][:, :, at:at + R1], src).then_inc(a1_high, 1)
                pool.wait_ge(a1_high, t + 1)
                pool.tensor_tensor(m1_b[LOW][:, :, at:at + R1], src,
                                   m1_b[HIGH][:, :, at:at + R1].bitcast(F32), ALU.subtract).then_inc(a1_placed, 1)

            split_exp_b(exp_b0_in, exp_b0_c, exp_b0_n)
            pool.wait_ge(a0_gathered, 16 * B)
            place_a0(0, 0)
            place_a0(1, 1)
            split_exp_b(exp_b1_in, exp_b1_c, exp_b1_n)
            pool.wait_ge(a1_gathered, 16 * B)
            for c in range(KC):
                pool.wait_ge(*high_of(F_M1[c] + 1))
                pool.tensor_tensor(m1_b[LOW][:, c, R1:R1 + NB], m1_f[:, c % 2, 0:NB],
                                   m1_b[HIGH][:, c, R1:R1 + NB].bitcast(F32), ALU.subtract).then_inc(m1_low, 1)
                pool.tensor_tensor(m1_a[LOW][:, c, :], m1_f[:, c % 2, NB:NCAT],
                                   m1_a[HIGH][:, c, :].bitcast(F32), ALU.subtract).then_inc(m1_low, 1)
            place_a1(0, 0)
            place_a1(1, 1)
            for p in range(1, PAIRS):
                for side in range(2):
                    t = 2 * p + side
                    pool.wait_ge(l0_scored, t - 1)
                    place_a0(t, side)
                for side in range(2):
                    t = 2 * p + side
                    pool.wait_ge(side_scored, t - 1)
                    place_a1(t, side)

        @block.tensor
        def _(pe):
            def turn(dst, src, k=P, start=True):
                return pe.matmul(dst, src, ident[0:k, 0:k], start=start, stop=True, is_transpose=True,
                                 skip_group_check=True)

            def products(dst, left, right, start, stop):
                for n, (a, b) in enumerate(PASSES):
                    last = pe.matmul(dst, left[a], right[b], start=start and n == 0, stop=stop and n == 2,
                                     skip_group_check=True)
                return last

            def fill(n):
                before = [k for k in range(n) if BANK_OF[k] == BANK_OF[n]]
                if before:
                    pe.wait_ge(*emptied(before[-1]))
                return banks[BANK_OF[n]]

            pe.wait_ge(const_step, 4)
            pe.wait_ge(exp_a0_in, 32)
            bank = fill(F_A0)
            for k in range(KC):
                last = turn(bank[:, k * P:(k + 1) * P], exp_a0_n[:, k:D:KC])
            last.then_inc(prep_filled, 1)
            bank = fill(F_ROUTE0)
            for k in range(KC):
                last = turn(bank[:, k * E:(k + 1) * E], route0_n[:, k:D:KC], E)
            last.then_inc(prep_filled, 1)
            pe.wait_ge(exp_a1_in, 32)
            bank = fill(F_A1)
            for k in range(KC):
                last = turn(bank[:, k * P:(k + 1) * P], exp_a1_n[:, k * P:(k + 1) * P])
            last.then_inc(prep_filled, 1)
            bank = fill(F_ROUTE1)
            for k in range(KC):
                last = turn(bank[:, k * E:(k + 1) * E], route1_n[:, k * P:(k + 1) * P], E)
            last.then_inc(prep_filled, 1)
            pe.wait_ge(*emptied(F_A0))
            pe.wait_ge(*emptied(F_ROUTE0))
            for half in w0_in:
                pe.wait_ge(half, 16)
            for n, chunks in ((F_M0, range(KC - 1)), (F_M0_G0, range(KC - 1, KC))):
                bank = fill(n)
                for c in chunks:
                    at = (c - chunks[0]) * SIDE
                    for k in range(KC):
                        last = pe.matmul(bank[:, at:at + SIDE], w0_n[:, k, c:D:KC], cat0_t[:, k, :],
                                         start=k == 0, stop=k == KC - 1, skip_group_check=True)
                if n == F_M0_G0:
                    pe.wait_ge(bias_placed, 1)
                    for k in range(KC):
                        last = pe.matmul(bank[0:U0, SIDE:2 * SIDE], lora_b0_n[:, k, :], cat0_t[:, k, :],
                                         start=k == 0, stop=k == KC - 1, skip_group_check=True)
                last.then_inc(prep_filled, 1)
            for j in range(KC):
                if j % 2 == 0:
                    pe.wait_ge(w_base_in[j // 2], 16)
                bank = fill(F_BASE + j)
                for k in range(KC):
                    last = turn(bank[:, k * P:(k + 1) * P], w_base_n[:, j, k * P:(k + 1) * P])
                last.then_inc(prep_filled, 1)

            def turn_exp_b(n, turned, src):
                pe.wait_ge(exp_b_split, turned)
                bank = fill(n)
                for c in range(KC):
                    last = turn(bank[:, c * P:(c + 1) * P], src[:, c, :])
                last.then_inc(prep_filled, 1)

            def turn_w1(c):
                if c % 2 == 0:
                    pe.wait_ge(w1_in[c // 2], 16)
                bank = fill(F_W1[c])
                for k in range(KC):
                    last = turn(bank[:, k * P:(k + 1) * P], w1_n[:, c, k * P:(k + 1) * P])
                last.then_inc(prep_filled, 1)

            def multiply_w1(c, n):
                a, b = BLOCKS[n]
                if n == 0:
                    pe.wait_ge(*low_of(F_W1[c]))
                bank = fill(F_M1[c] + n)
                for k in range(KC):
                    last = products(bank[:, 0:b - a], [t[:, c % 2, k, :] for t in w1_t],
                                    [t[:, k, a:b] for t in cat1_t], k == 0, k == KC - 1)
                last.then_inc(prep_filled, 1)

            def multiply_lora_b1():
                pe.wait_ge(*low_of(F_LORA_B1))
                for n, (a, b) in enumerate(BLOCKS):
                    bank = fill(F_G1 + n)
                    for k in range(KC):
                        last = products(bank[:, 0:b - a], [t[:, k, :] for t in lora_b1_t],
                                        [t[:, k, a:b] for t in cat1_t], k == 0, k == KC - 1)
                    last.then_inc(prep_filled, 1)

            bank_xt = (bank_x, bank_l0[1])

            def turn_x(q, side):
                if side == 0:
                    pe.wait_ge(x_loaded, 16 * (q + 1))
                if q > 0:
                    if side == 0:
                        pe.wait_ge(x1_summed, 2 * q - 1)
                    else:
                        pe.wait_ge(gated0t_low, 2 * q)
                for c in range(KC):
                    last = turn(bank_xt[side][:, c * P:(c + 1) * P], x_in[:, side, c:D:KC])
                last.then_inc(xt_filled, 1)

            def score0(q, side):
                t = 2 * q + side
                pe.wait_ge(xt_copied, t + 1)
                pe.wait_ge(a0_placed, t + 1)
                if q > 0 and side == 0:
                    pe.wait_ge(x1_summed, 2 * q)
                for c in range(KC):
                    last = pe.matmul(bank_l0[side][:, 0:N0], x_t[q % 2][:, c, side, :], m0[side][:, c, :],
                                     start=c == 0, stop=c == KC - 1, skip_group_check=True)
                last.then_inc(l0_scored, 1)

            def turn_u0(q, side):
                pe.wait_ge(u0_copied, 2 * q + side + 1)
                turn(bank_l0[side][0:U0, U0_T:U0_T + P], u0[:, side, :], start=False).then_inc(u0t_filled, 1)

            def adapt0(q, side):
                pe.wait_ge(u0t_copied, 2 * q + side + 1)
                pe.matmul(bank_l0[side][:, 0:SIDE], u0_t[:, side, :], g0[:, :], start=False, stop=True,
                          skip_group_check=True).then_inc(l0_ready, 1)

            def turn_gated0(q, side):
                pe.wait_ge(gated0_ready, 2 * q + side + 1)
                turn(bank_l0[side][:, GATED0_T:GATED0_T + P], gated0[:, side, :], start=False
                     ).then_inc(gated0t_filled, 1)

            def ffn0(q):
                pe.wait_ge(gated0t_low, 2 * q + 2)
                for r, bank in enumerate((bank_x, bank_l0[0])):
                    for j in range(2):
                        c = 2 * r + j
                        last = products(bank[:, j * 2 * P:(j + 1) * 2 * P], [w[:, c, :] for w in exp_b0_t],
                                        [g[:, :, :] for g in gated0_t], True, True)
                    last.then_inc(x1_filled, 1)

            def side1(p, side, chunks):
                t = 2 * p + side
                if chunks[0] == 0:
                    pe.wait_ge(a1_placed, t + 1)
                    if p > 0:
                        pe.wait_ge(y_ready, t - 1)
                a = 0 if side == 0 else R1
                for c in chunks:
                    if side == 0 and c % 2 == 0:
                        pe.wait_ge(x1_low, 2 * p + c // 2 + 1)
                    last = products(acc[side][:, 0:R1 + NB], [v[:, c, side, :] for v in x1_t[p % 2]],
                                    [m[:, c, a:a + R1 + NB] for m in m1_b], c == 0, c == KC - 1)
                if chunks[-1] == KC - 1:
                    last.then_inc(side_scored, 1)

            def base1(p, side):
                for c in range(KC):
                    products(acc[side][:, 512:512 + HB], [v[:, c, side, :] for v in x1_t[p % 2]],
                             [m[:, c, :] for m in m1_a], c == 0, False)

            def turn_u1(p, side):
                t = 2 * p + side
                pe.wait_ge(u1_copied, t + 1)
                if t > 0:
                    pe.wait_ge(gated1t_low, t)
                turn(bank_small[:, side * P:(side + 1) * P], u1[:, side, :, :]).then_inc(u1t_filled, 1)

            def adapt_side1(p, side):
                pe.wait_ge(u1t_low, 2 * p + side + 1)
                at = SIDE_AT[side]
                products(acc[side][:, at:at + NB], [u[:, side, :] for u in u1_t], [g[:, 0:NB] for g in g1],
                         False, False).then_inc(l1_ready, 1)

            def adapt_base1(p, side):
                products(acc[side][:, 512:512 + HB], [u[:, side, :] for u in u1_t], [g[:, NB:NCAT] for g in g1],
                         False, False)

            def turn_gated1(p, side):
                t = 2 * p + side
                pe.wait_ge(gated1_ready, t + 1)
                turn(bank_small[:, (2 + side) * P:(3 + side) * P], gated1[:, side, :]).then_inc(gated1t_filled, 1)

            def ffn1(p, side):
                pe.wait_ge(gated1t_low, 2 * p + side + 1)
                left = [g[:, side, :] for g in gated1_t]
                at = SIDE_AT[side] + SIDE
                wide = [e[:, :, :].rearrange("p a c -> p (a c)") for e in exp_b1_t]
                products(acc[side][:, at:at + HB], left, [w[:, 0:HB] for w in wide], False, True)
                products(acc[side][:, 512:512 + HB], left, [w[:, HB:D] for w in wide], False, True
                         ).then_inc(y_filled, 1)

            turn_x(0, 0)
            turn_x(0, 1)
            turn_exp_b(F_B0, 1, exp_b0_c)
            turn_w1(0)
            turn_w1(1)
            pe.wait_ge(m0_copied, 1)
            score0(0, 0)
            multiply_w1(0, 0)
            score0(0, 1)
            multiply_w1(0, 1)
            turn_u0(0, 0)
            turn_u0(0, 1)
            turn_w1(2)
            multiply_w1(1, 0)
            adapt0(0, 0)
            adapt0(0, 1)
            multiply_w1(1, 1)
            turn_gated0(0, 0)
            turn_w1(3)
            multiply_w1(2, 0)
            turn_gated0(0, 1)
            multiply_w1(2, 1)
            pe.wait_ge(*low_of(F_B0))
            ffn0(0)
            multiply_w1(3, 0)
            multiply_w1(3, 1)
            pe.wait_ge(b1_gathered, 16 * B)
            bank = fill(F_LORA_B1)
            for k in range(KC):
                last = turn(bank[:, k * P:(k + 1) * P], lora_b1_g[:, k * P:(k + 1) * P])
            last.then_inc(prep_filled, 1)
            turn_exp_b(F_B1, 2, exp_b1_c)
            multiply_lora_b1()
            pe.wait_ge(m1_low, 2 * KC)
            for p in range(PAIRS):
                q = p + 1
                more = q < PAIRS
                side1(p, 0, range(KC))
                if more:
                    turn_x(q, 0)
                    turn_x(q, 1)
                if p > 0:
                    turn_gated1(p - 1, 1)
                    ffn1(p - 1, 1)
                turn_u1(p, 0)
                if more:
                    score0(q, 0)
                if p == 0:
                    pe.wait_ge(*low_of(F_G1 + 1))
                adapt_side1(p, 0)
                if more:
                    score0(q, 1)
                    turn_u0(q, 0)
                side1(p, 1, range(KC // 2))
                if more:
                    turn_u0(q, 1)
                    adapt0(q, 0)
                side1(p, 1, range(KC // 2, KC))
                if more:
                    adapt0(q, 1)
                turn_gated1(p, 0)
                base1(p, 0)
                adapt_base1(p, 0)
                turn_u1(p, 1)
                if more:
                    turn_gated0(q, 0)
                    turn_gated0(q, 1)
                ffn1(p, 0)
                if more:
                    ffn0(q)
                adapt_side1(p, 1)
                base1(p, 1)
                adapt_base1(p, 1)
            turn_gated1(PAIRS - 1, 1)
            ffn1(PAIRS - 1, 1)

        @block.scalar
        def _(act):
            def blocks(n, count, w):
                return banks[BANK_OF[n]][:, 0:count * w].rearrange("p (k w) -> p k w", k=count)

            def copy(dst, src, **more):
                return act.activation(dst, src, ACT.Copy, **more)

            def filled(n):
                act.wait_ge(prep_filled, n + 1)

            filled(F_A0)
            copy(cat0_t[:, :, 0:ER], blocks(F_A0, KC, P)).then_inc(prep_high, 1)
            filled(F_A1)
            copy(cat1_t[HIGH][:, :, 0:ER], blocks(F_A1, KC, P)).then_inc(prep_high, 1)
            filled(F_ROUTE1)
            copy(cat1_t[HIGH][:, :, ER:SIDE], blocks(F_ROUTE1, KC, E)).then_inc(prep_high, 1)
            filled(F_M0)
            copy(m0[0][:, 0:KC - 1, 0:SIDE], blocks(F_M0, KC - 1, SIDE)).then_inc(prep_high, 1)
            filled(F_M0_G0)
            copy(m0[0][:, KC - 1, 0:SIDE], banks[BANK_OF[F_M0_G0]][:, 0:SIDE])
            copy(g0[:, :], banks[BANK_OF[F_M0_G0]][0:U0, SIDE:2 * SIDE]).then_inc(prep_high, 1)
            for j in range(KC):
                filled(F_BASE + j)
                copy(cat1_t[HIGH][:, :, SIDE + j * P:SIDE + (j + 1) * P], blocks(F_BASE + j, KC, P)).then_inc(prep_high, 1)

            def high_w1(c):
                filled(F_W1[c])
                copy(w1_t[HIGH][:, c % 2, :, :], blocks(F_W1[c], KC, P)).then_inc(prep_high, 1)

            def high_m1(c, n):
                a, b = BLOCKS[n]
                act.wait_ge(*low_of(F_M1[c] + n))
                copy(m1_b[HIGH][:, c, R1:R1 + NB] if n == 0 else m1_a[HIGH][:, c, :], m1_f[:, c % 2, a:b]
                     ).then_inc(prep_high, 1)

            def copy_xt(q, side):
                act.wait_ge(xt_filled, 2 * q + side + 1)
                copy(x_t[q % 2][:, :, side, :], (bank_x, bank_l0[1])[side][:, :].rearrange("p (c t) -> p c t", c=KC)).then_inc(xt_copied, 1)

            def copy_u0(q, side):
                act.wait_ge(l0_scored, 2 * q + side + 1)
                copy(u0[:, side, 0:R0], bank_l0[side][:, SIDE:N0], scale=SCALE0).then_inc(u0_copied, 1)

            def copy_u0t(q, side):
                act.wait_ge(u0t_filled, 2 * q + side + 1)
                copy(u0_t[:, side, :], bank_l0[side][0:U0, U0_T:U0_T + P]).then_inc(u0t_copied, 1)

            def high_gated0(q, side):
                act.wait_ge(gated0t_filled, 2 * q + side + 1)
                copy(gated0_t[HIGH][:, side, :], bank_l0[side][:, GATED0_T:GATED0_T + P]).then_inc(gated0t_high, 1)

            def high_x1(q, r):
                act.wait_ge(x1_summed, 2 * q + r + 1)
                copy(x1_t[q % 2][HIGH][:, 2 * r:2 * r + 2, :, :], x1_f[:, 2 * r:2 * r + 2, :, :]).then_inc(x1_high, 1)

            def copy_u1(p, side):
                act.wait_ge(side_scored, 2 * p + side + 1)
                at = U1_AT[side]
                copy(u1[:, side, :, :], acc[side][:, at:at + R1].unsqueeze(1).to_broadcast([P, B, R1])
                     ).then_inc(u1_copied, 1)

            def high_u1(p, side):
                t = 2 * p + side
                act.wait_ge(u1t_filled, t + 1)
                copy(u1_t[HIGH][:, side, :], bank_small[:, side * P:(side + 1) * P],
                     scale=own_batch[:, bass.ds(t, 1)]).then_inc(u1t_high, 1)

            def exp1(p, side):
                act.wait_ge(below_ready, 2 * p + side + 1)
                act.activation(expo[:, side, :], below[:, side, :], ACT.Exp).then_inc(expo_ready, 1)

            def high_gated1(p, side):
                act.wait_ge(gated1t_filled, 2 * p + side + 1)
                copy(gated1_t[HIGH][:, side, :], bank_small[:, (2 + side) * P:(3 + side) * P]).then_inc(gated1t_high, 1)

            copy_xt(0, 0)
            copy_xt(0, 1)
            filled(F_B0)
            copy(exp_b0_t[HIGH][:, :, :], blocks(F_B0, KC, P)).then_inc(prep_high, 1)
            high_w1(0)
            high_w1(1)
            copy_u0(0, 0)
            high_m1(0, 0)
            copy_u0(0, 1)
            high_m1(0, 1)
            copy_u0t(0, 0)
            copy_u0t(0, 1)
            high_w1(2)
            high_m1(1, 0)
            high_m1(1, 1)
            high_gated0(0, 0)
            high_w1(3)
            high_m1(2, 0)
            high_gated0(0, 1)
            high_m1(2, 1)
            high_x1(0, 0)
            high_x1(0, 1)
            high_m1(3, 0)
            high_m1(3, 1)
            filled(F_LORA_B1)
            copy(lora_b1_t[HIGH][:, :, :], blocks(F_LORA_B1, KC, P)).then_inc(prep_high, 1)
            filled(F_B1)
            copy(exp_b1_t[HIGH][:, :, :].rearrange("p a c -> p c a"), blocks(F_B1, KC, P), scale=SCALE_FFN1
                 ).then_inc(prep_high, 1)
            for n, (a, b) in enumerate(BLOCKS):
                filled(F_G1 + n)
                copy(g1[HIGH][:, a:b], banks[BANK_OF[F_G1 + n]][:, 0:b - a]).then_inc(prep_high, 1)
            for p in range(PAIRS):
                q = p + 1
                more = q < PAIRS
                copy_u1(p, 0)
                if more:
                    copy_xt(q, 0)
                if p > 0:
                    high_gated1(p - 1, 1)
                if more:
                    copy_xt(q, 1)
                high_u1(p, 0)
                if more:
                    copy_u0(q, 0)
                exp1(p, 0)
                if more:
                    copy_u0(q, 1)
                    copy_u0t(q, 0)
                    copy_u0t(q, 1)
                copy_u1(p, 1)
                high_gated1(p, 0)
                high_u1(p, 1)
                if more:
                    high_gated0(q, 0)
                    high_gated0(q, 1)
                    high_x1(q, 0)
                    high_x1(q, 1)
                exp1(p, 1)
            high_gated1(PAIRS - 1, 1)

        @block.vector
        def _(dve):
            def blocks(n, count, w):
                return banks[BANK_OF[n]][:, 0:count * w].rearrange("p (k w) -> p k w", k=count)

            def low(dst, exact, high):
                return dve.tensor_tensor(dst, exact, high.bitcast(F32), ALU.subtract)

            steps = [0]

            def finished(ins):
                steps[0] += 1
                ins.then_inc(dve_step, 1)
                dve.wait_ge(dve_step, steps[0])

            dve.wait_ge(prep_filled, F_ROUTE0 + 1)
            dve.tensor_copy(cat0_t[:, :, ER:SIDE], blocks(F_ROUTE0, KC, E)).then_inc(prep_low, 1)
            dve.wait_ge(*high_of(F_A1))
            low(cat1_t[LOW][:, :, 0:ER], blocks(F_A1, KC, P), cat1_t[HIGH][:, :, 0:ER]).then_inc(prep_low, 1)
            dve.wait_ge(*high_of(F_ROUTE1))
            low(cat1_t[LOW][:, :, ER:SIDE], blocks(F_ROUTE1, KC, E), cat1_t[HIGH][:, :, ER:SIDE]).then_inc(prep_low, 1)
            dve.wait_ge(*high_of(F_M0_G0))
            dve.tensor_copy(m0[1][:, :, 0:SIDE], m0[0][:, :, 0:SIDE]).then_inc(m0_copied, 1)
            for j in range(KC):
                a, b = SIDE + j * P, SIDE + (j + 1) * P
                dve.wait_ge(*high_of(F_BASE + j))
                low(cat1_t[LOW][:, :, a:b], blocks(F_BASE + j, KC, P), cat1_t[HIGH][:, :, a:b]).then_inc(prep_low, 1)
            dve.wait_ge(*high_of(F_B0))
            low(exp_b0_t[LOW][:, :, :], blocks(F_B0, KC, P), exp_b0_t[HIGH][:, :, :]).then_inc(prep_low, 1)

            def low_w1(c):
                dve.wait_ge(*high_of(F_W1[c]))
                low(w1_t[LOW][:, c % 2, :, :], blocks(F_W1[c], KC, P), w1_t[HIGH][:, c % 2, :, :]).then_inc(prep_low, 1)

            def sum_m1(c, n):
                if c >= 2 and n == 0:
                    dve.wait_ge(*high_of(F_M1[c - 2] + 1))
                    dve.wait_ge(m1_low, 2 * (c - 1))
                a, b = BLOCKS[n]
                at = KC - 1 - c
                dve.wait_ge(prep_filled, F_M1[c] + n + 1)
                dve.tensor_tensor(m1_f[:, c % 2, a:b], banks[BANK_OF[F_M1[c] + n]][:, 0:b - a],
                                  diag[:, at + a:at + b], ALU.add).then_inc(prep_low, 1)

            def route0(q, side):
                t = 2 * q + side
                scores = bank_l0[side][:, ER:SIDE]
                dve.wait_ge(l0_ready, t + 1)
                finished(dve.max(top0[:, side, :], scores))
                finished(dve.max_index(top0_at[:, side, :], top0[:, side, :], scores))
                finished(dve.scalar_tensor_tensor(out=gate0[:, side, :], in0=expert_no[:, :], scalar=top0_at[:, side, 0:1],
                                                  in1=scores, op0=ALU.is_equal, op1=ALU.mult))
                dve.tensor_tensor(gated0[:, side, :].rearrange("p (e r) -> p e r", e=E),
                                  bank_l0[side][:, 0:ER].rearrange("p (e r) -> p e r", e=E),
                                  gate0[:, side, :].unsqueeze(2).to_broadcast([P, E, RE]), ALU.mult
                                  ).then_inc(gated0_ready, 1)

            def low_gated0(q, side):
                dve.wait_ge(gated0t_high, 2 * q + side + 1)
                low(gated0_t[LOW][:, side, :], bank_l0[side][:, GATED0_T:GATED0_T + P], gated0_t[HIGH][:, side, :]
                    ).then_inc(gated0t_low, 1)

            def sum_x1(q, r):
                dve.wait_ge(x1_filled, 2 * q + r + 1)
                dve.tensor_tensor(x1_f[:, 2 * r:2 * r + 2, :, :],
                                  (bank_x, bank_l0[0])[r][:, :].rearrange("p (c s t) -> p c s t", c=2, s=2),
                                  x_t[q % 2][:, 2 * r:2 * r + 2, :, :], ALU.add).then_inc(x1_summed, 1)

            def low_x1(q, r):
                dve.wait_ge(x1_high, 2 * q + r + 1)
                low(x1_t[q % 2][LOW][:, 2 * r:2 * r + 2, :, :], x1_f[:, 2 * r:2 * r + 2, :, :],
                    x1_t[q % 2][HIGH][:, 2 * r:2 * r + 2, :, :]).then_inc(x1_low, 1)

            def low_u1(p, side):
                t = 2 * p + side
                dve.wait_ge(u1t_high, t + 1)
                dve.scalar_tensor_tensor(out=u1_t[LOW][:, side, :], in0=bank_small[:, side * P:(side + 1) * P],
                                         scalar=own_batch[:, bass.ds(t, 1)], in1=u1_t[HIGH][:, side, :].bitcast(F32),
                                         op0=ALU.mult, op1=ALU.subtract).then_inc(u1t_low, 1)

            def route1(p, side):
                t = 2 * p + side
                at = SIDE_AT[side]
                scores = acc[side][:, at + ER:at + SIDE]
                dve.wait_ge(l1_ready, t + 1)
                finished(dve.max(top1[:, side, :], scores))
                dve.tensor_scalar(below[:, side, :], scores, top1[:, side, 0:1], None, ALU.subtract).then_inc(below_ready, 1)
                finished(dve.max_index(top1_at[:, side, :], top1[:, side, :], scores))
                finished(dve.tensor_scalar(first[:, side, :], expert_no[:, :], top1_at[:, side, 0:1], None, ALU.is_equal))
                finished(dve.scalar_tensor_tensor(out=chosen[:, side, :], in0=expert_no[:, :], scalar=top1_at[:, side, 1:2],
                                                  in1=first[:, side, :], op0=ALU.is_equal, op1=ALU.add))
                dve.wait_ge(expo_ready, t + 1)
                finished(dve.scalar_tensor_tensor(out=weight[:, side, :], in0=chosen[:, side, :], scalar=1.0,
                                                  in1=expo[:, side, :], op0=ALU.mult, op1=ALU.mult,
                                                  accum_out=total[:, side:side + 1]))
                finished(dve.reciprocal(inverse[:, side:side + 1], total[:, side:side + 1]))
                dve.scalar_tensor_tensor(out=gated1[:, side, :].rearrange("p (e r) -> p e r", e=E),
                                         in0=acc[side][:, at:at + ER].rearrange("p (e r) -> p e r", e=E),
                                         scalar=inverse[:, side:side + 1],
                                         in1=weight[:, side, :].unsqueeze(2).to_broadcast([P, E, RE]),
                                         op0=ALU.mult, op1=ALU.mult).then_inc(gated1_ready, 1)

            def low_gated1(p, side):
                dve.wait_ge(gated1t_high, 2 * p + side + 1)
                low(gated1_t[LOW][:, side, :], bank_small[:, (2 + side) * P:(3 + side) * P], gated1_t[HIGH][:, side, :]
                    ).then_inc(gated1t_low, 1)

            def sum_y(p, side):
                t = 2 * p + side
                dve.wait_ge(y_filled, t + 1)
                if p > 0:
                    dve.wait_ge(stored[side], 16 * p)
                dve.tensor_tensor(y[:, side, :].rearrange("p (a b) -> p a b", a=2), base_part(side),
                                  b_base_all[:, :].rearrange("p (a b) -> p a b", a=2), ALU.add).then_inc(y_ready, 1)

            low_w1(0)
            low_w1(1)
            dve.wait_ge(const_step, 9)
            sum_m1(0, 0)
            sum_m1(0, 1)
            low_w1(2)
            sum_m1(1, 0)
            route0(0, 0)
            route0(0, 1)
            sum_m1(1, 1)
            low_gated0(0, 0)
            low_w1(3)
            sum_m1(2, 0)
            low_gated0(0, 1)
            sum_m1(2, 1)
            sum_x1(0, 0)
            sum_x1(0, 1)
            low_x1(0, 0)
            low_x1(0, 1)
            sum_m1(3, 0)
            sum_m1(3, 1)
            dve.wait_ge(*high_of(F_LORA_B1))
            low(lora_b1_t[LOW][:, :, :], blocks(F_LORA_B1, KC, P), lora_b1_t[HIGH][:, :, :]).then_inc(prep_low, 1)
            dve.wait_ge(*high_of(F_B1))
            dve.scalar_tensor_tensor(out=exp_b1_t[LOW][:, :, :].rearrange("p a c -> p c a"), in0=blocks(F_B1, KC, P),
                                     scalar=SCALE_FFN1,
                                     in1=exp_b1_t[HIGH][:, :, :].bitcast(F32).rearrange("p a c -> p c a"),
                                     op0=ALU.mult, op1=ALU.subtract).then_inc(prep_low, 1)
            for n, (a, b) in enumerate(BLOCKS):
                dve.wait_ge(*high_of(F_G1 + n))
                low(g1[LOW][:, a:b], banks[BANK_OF[F_G1 + n]][:, 0:b - a], g1[HIGH][:, a:b]).then_inc(prep_low, 1)
            dve.wait_ge(b_base_in, 16)
            for p in range(PAIRS):
                q = p + 1
                more = q < PAIRS
                if p > 0:
                    low_gated1(p - 1, 1)
                    sum_y(p - 1, 1)
                low_u1(p, 0)
                route1(p, 0)
                if more:
                    route0(q, 0)
                low_gated1(p, 0)
                if more:
                    route0(q, 1)
                low_u1(p, 1)
                if more:
                    low_gated0(q, 0)
                    low_gated0(q, 1)
                sum_y(p, 0)
                if more:
                    sum_x1(q, 0)
                    sum_x1(q, 1)
                    low_x1(q, 0)
                    low_x1(q, 1)
                route1(p, 1)
            low_gated1(PAIRS - 1, 1)
            sum_y(PAIRS - 1, 1)


_INS = ["x", "itok_B_0_4", "itok_B_0_15", "L0_cond_weight", "L0_cond_bias", "L0_cond_lora_A", "L0_cond_lora_B",
        "L0_ffn_route_w", "L0_ffn_A", "L0_ffn_Bw", "L1_cond_W", "L1_cond_lora_A", "L1_cond_lora_B", "L1_ffn_W_base",
        "L1_ffn_b_base", "L1_ffn_W_router", "L1_ffn_A_stack", "L1_ffn_B_stack"]


def kernel(**inputs):
    import numpy as _np
    import concourse.bacc as _bacc
    from concourse import mybir as _mybir
    from concourse.bass_utils import run_bass_kernel_spmd as _run

    nc = _bacc.Bacc("TRN2", target_bir_lowering=False, num_devices=1)
    arrays, args = {}, []
    for name in _INS:
        a = _np.ascontiguousarray(inputs[name])
        arrays[f"in_{name}_dram"] = a
        args.append(nc.dram_tensor(f"in_{name}_dram", a.shape, _mybir.dt.from_np(a.dtype), kind="ExternalInput").ap())
    out = nc.dram_tensor("out_0_dram", inputs["x"].shape, _mybir.dt.float32, kind="ExternalOutput").ap()
    adaln_ffn_kernel(nc, *args, out)
    r = _run(nc, [arrays], core_ids=[0])
    return r.results[0]["out_0_dram"]
```

```python
from contextlib import ExitStack

import concourse.bass as bass
from concourse import mybir

F32 = mybir.dt.float32
F32R = mybir.dt.float32r
I32 = mybir.dt.int32
U32 = mybir.dt.uint32
ALU = mybir.AluOpType
ACT = mybir.ActivationFunctionType

P = 128
HIGH, LOW = 0, 1
PASSES = ((HIGH, HIGH), (HIGH, LOW), (LOW, HIGH))


def adaln_ffn_kernel(nc, x_turned, labels, w0_cat0, lora_a0, exp_b, cat1_w1, lora1, b_base, out):
    B, S, D = out.shape
    L0, _, _, R0 = lora_a0.shape
    L1, _, _, _, R1 = lora1.shape
    RE = R1
    KC = D // P
    ER = exp_b.shape[0]
    E = ER // RE
    SIDE = ER + E
    N0 = SIDE + R0
    U0 = R0 + 1
    HB = D // 2
    NB = SIDE + HB
    NCAT = SIDE + D
    WB = R1 + NB + R1
    BR = B * R1
    BLOCKS = ((0, NB), (NB, NCAT))
    PAIRS = B // 2
    SCALE0 = 16 / 32
    SCALE_FFN1 = 32.0 / 16
    U1 = len(PASSES) * R1
    NW = NCAT + D
    NFIRST = NCAT + HB
    assert S == P and ER == P and BR == P and D == 4 * P
    assert w0_cat0.shape == (P, KC, D + SIDE + U0) and cat1_w1.shape == (P, KC, NW)

    with ExitStack() as ctx:
        def sb(name, shape, dt=F32):
            return ctx.enter_context(nc.sbuf_tensor(name, shape, dt))

        def sem(name):
            return ctx.enter_context(nc.semaphore(name))

        ident = sb("ident", [P, P])
        diag = sb("diag", [P, NCAT + KC - 1])
        expert_no = sb("expert_no", [P, E])
        w0_cat0_n = sb("w0_cat0_n", [P, KC, D + SIDE + U0])
        exp_b_n = sb("exp_b_n", [ER, 2, D])
        cat1_w1_n = sb("cat1_w1_n", [P, KC, NW])
        b_base_all = sb("b_base_all", [P, D])
        labels_n = sb("labels_n", [1, 2, B], I32)
        lora_a0_g = sb("lora_a0_g", [P, B, KC, R0])
        lora1_g = sb("lora1_g", [P, B, 2, KC, R1])
        m0 = [sb(f"m0_{s}", [P, KC, N0]) for s in range(2)]
        g0 = sb("g0", [U0, SIDE])
        exp_b0_s = [sb(f"exp_b0_s{h}", [ER, KC, P], F32R) for h in range(2)]
        exp_b1_s = [sb(f"exp_b1_s{h}", [ER, D], F32R) for h in range(2)]
        lora_b1_s = [sb(f"lora_b1_s{h}", [P, KC, R1, B], F32R) for h in range(2)]
        cat1_w1_s = [sb(f"cat1_w1_s{h}", [P, KC, NW], F32R) for h in range(2)]
        g1 = [sb(f"g1_{h}", [BR, NCAT], F32R) for h in range(2)]
        g1_stack = sb("g1_stack", [U1, B, NCAT], F32R)
        m1_f = sb("m1_f", [P, 2, NCAT])
        m1_b = [sb(f"m1_b{h}", [P, KC, WB], F32R) for h in range(2)]
        m1_a = [sb(f"m1_a{h}", [P, KC, HB], F32R) for h in range(2)]
        x_t = [sb(f"x_t{i}", [P, KC, 2, P]) for i in range(2)]
        x1_f = sb("x1_f", [P, KC, 2, P])
        x1_t = [[sb(f"x1_t{i}_{h}", [P, KC, 2, P], F32R) for h in range(2)] for i in range(2)]
        u0 = sb("u0", [P, 2, U0])
        u0_t = sb("u0_t", [U0, 2, P])
        top0 = sb("top0", [P, 2, 8])
        top0_at = sb("top0_at", [P, 2, 8], U32)
        gate0 = sb("gate0", [P, 2, E])
        gated0 = sb("gated0", [P, 2, ER])
        gated0_t = [sb(f"gated0_t{h}", [ER, 2, P], F32R) for h in range(2)]
        u1 = sb("u1", [P, 2, len(PASSES), R1])
        u1_t = sb("u1_t", [U1, 2, P], F32R)
        top1 = sb("top1", [P, 2, 8])
        top1_at = sb("top1_at", [P, 2, 8], U32)
        below = sb("below", [P, 2, E])
        expo = sb("expo", [P, 2, E])
        first = sb("first", [P, 2, E])
        chosen = sb("chosen", [P, 2, E])
        weight = sb("weight", [P, 2, E])
        total = sb("total", [P, 2])
        inverse = sb("inverse", [P, 2])
        gated1 = sb("gated1", [P, 2, ER])
        gated1_t = [sb(f"gated1_t{h}", [ER, 2, P], F32R) for h in range(2)]
        y = sb("y", [P, 3, D])

        bank_x1_u1 = ctx.enter_context(nc.psum_tensor("bank_x1_u1", [P, 512], F32))
        bank_gated1 = ctx.enter_context(nc.psum_tensor("bank_gated1", [P, 512], F32))
        layer0 = ctx.enter_context(nc.psum_tensor("layer0", [P, 1024], F32))
        acc = [ctx.enter_context(nc.psum_tensor(f"acc_{s}", [P, 1024], F32)) for s in range(2)]
        bank_l0 = [layer0[:, 0:512], layer0[:, 512:1024]]
        banks = [bank_x1_u1[:, :], bank_l0[0], bank_l0[1], bank_gated1[:, :],
                 acc[0][:, 0:512], acc[0][:, 512:1024], acc[1][:, 0:512], acc[1][:, 512:1024]]

        def acc_of(t):
            return layer0 if t == B - 1 else acc[t % 2]

        U0_T, GATED0_T = N0, N0 + P
        SIDE_AT = (R1, 0)
        U1_AT = (0, NB)
        A1_AT = (0, R1 + NB)

        def y_slot(t):
            return 2 if t == B - 1 else t % 2

        def base_part(t):
            at = SIDE_AT[t % 2] + SIDE
            w = 512 - at
            return acc_of(t)[:, at:at + 2 * w].rearrange("p (a b) -> p a b", a=2)[:, :, 0:HB]

        labels_in, x_loaded, exp_b_in, b_base_in, lora1_gathered, w1_rest_in = (
            sem(n) for n in ("labels_in", "x_loaded", "exp_b_in", "b_base_in", "lora1_gathered",
                             "w1_rest_in"))
        w0_cat0_in = [sem(f"w0_cat0_in_{k}") for k in range(KC)]
        cat1_w1_in = [sem(f"cat1_w1_in_{k}") for k in range(KC)]
        a0_gathered = [sem(f"a0_gathered_{p}") for p in range(PAIRS)]
        const_step, m0_copied, a0_placed, a1_high, a1_placed, g1_stacked = (
            sem(n) for n in ("const_step", "m0_copied", "a0_placed", "a1_high", "a1_placed", "g1_stacked"))
        cat1_w1_high, cat1_w1_low, lora_b1_high, lora_b1_low, exp_b0_high, exp_b0_low, exp_b1_high, exp_b1_low = (
            sem(n) for n in ("cat1_w1_high", "cat1_w1_low", "lora_b1_high", "lora_b1_low", "exp_b0_high", "exp_b0_low",
                             "exp_b1_high", "exp_b1_low"))
        stored = [sem(f"stored_{s}") for s in range(2)]
        prep_filled, prep_high, prep_low, m1_low = (sem(n) for n in ("prep_filled", "prep_high", "prep_low", "m1_low"))
        l0_scored, u0_copied, u0t_filled, u0t_copied, l0_ready = (
            sem(n) for n in ("l0_scored", "u0_copied", "u0t_filled", "u0t_copied", "l0_ready"))
        gated0_ready, gated0t_filled, gated0t_high, gated0t_low, x1_filled, x1_summed, x1_high, x1_low = (
            sem(n) for n in ("gated0_ready", "gated0t_filled", "gated0t_high", "gated0t_low", "x1_filled", "x1_summed",
                             "x1_high", "x1_low"))
        side_scored, u1_copied, u1t_filled, u1t_high, u1t_low, l1_ready = (
            sem(n) for n in ("side_scored", "u1_copied", "u1t_filled", "u1t_high", "u1t_low", "l1_ready"))
        below_ready, expo_ready, gated1_ready, gated1t_filled, gated1t_high, gated1t_low, y_filled, y_ready, dve_step = (
            sem(n) for n in ("below_ready", "expo_ready", "gated1_ready", "gated1t_filled", "gated1t_high", "gated1t_low",
                             "y_filled", "y_ready", "dve_step"))

        F_M0, F_M0_G0 = 0, 1
        F_M1 = ((2, 3), (4, 5), (6, 7), (10, 11))
        F_G1 = 8
        BANK_OF = (1, 3, 4, 5, 6, 7, 4, 5, 6, 7, 6, 7)
        NOT_ON_DVE = (F_M0, F_M0_G0)
        FIRST = 2

        def high_of(n):
            return prep_high, n + 1

        def low_of(n):
            return prep_low, sum(k not in NOT_ON_DVE for k in range(n + 1))

        def emptied(n):
            return high_of(n) if n in NOT_ON_DVE else low_of(n)

        block = ctx.enter_context(nc.Block())

        @block.sync
        def _(sp):
            def load_x(q):
                if q >= 2:
                    sp.wait_ge(x1_summed, 2 * (q - 1))
                sp.dma_start(x_t[q % 2][:, :, :, :], x_turned[q]).then_inc(x_loaded, 16)

            def load_cat1_w1(k):
                sp.dma_start(cat1_w1_n[:, k, 0:NFIRST], cat1_w1[:, k, 0:NFIRST]).then_inc(cat1_w1_in[k], 16)

            for k in range(KC):
                sp.dma_start(w0_cat0_n[:, k, :], w0_cat0[:, k, :]).then_inc(w0_cat0_in[k], 16)
                if k == 0:
                    sp.dma_start(labels_n[0:1, :, :], labels.rearrange("(a l) b -> a l b", a=1)).then_inc(labels_in, 16)
            load_cat1_w1(0)
            load_x(0)
            load_cat1_w1(1)
            sp.wait_ge(labels_in, 16)
            _, named0 = nc.values_load_multi_w_load_instructions(
                labels_n[0:1, 0, :], engines=(mybir.EngineType.SP,), min_val=0, max_val=L0 - 1)
            _, named1 = nc.values_load_multi_w_load_instructions(
                labels_n[0:1, 1, :], engines=(mybir.EngineType.SP,), min_val=0, max_val=L1 - 1)

            def gather_a0(b):
                sp.dma_start(lora_a0_g[:, b:b + 1, :, :],
                             lora_a0[bass.ds(named0[b], 1)].rearrange("a p c r -> p a c r")
                             ).then_inc(a0_gathered[b // 2], 16)

            gather_a0(0)
            gather_a0(1)
            for k in range(2, KC):
                load_cat1_w1(k)
            sp.dma_start(cat1_w1_n[:, :, NFIRST:NW], cat1_w1[:, :, NFIRST:NW]).then_inc(w1_rest_in, 16)
            sp.dma_start(exp_b_n[:, :, :], exp_b).then_inc(exp_b_in, 16)
            for b in range(B):
                sp.dma_start(lora1_g[:, b:b + 1, :, :, :],
                             lora1[bass.ds(named1[b], 1)].rearrange("a p m c r -> p a m c r")
                             ).then_inc(lora1_gathered, 16)
            load_x(1)
            for b in range(2, B):
                gather_a0(b)
            sp.dma_start(b_base_all[:, :], b_base.rearrange("(a n) -> a n", a=1).to_broadcast([P, D])).then_inc(b_base_in, 16)

            load_x(2)
            sp.wait_ge(*low_of(F_G1 + 1))
            for n, (_, part) in enumerate(PASSES):
                sp.dma_start(g1_stack[n * R1:(n + 1) * R1, :, :].bitcast(F32), g1[part][:, :].bitcast(F32)
                             ).then_inc(g1_stacked, 16)
            for p in range(PAIRS):
                if p + 3 < PAIRS:
                    load_x(p + 3)
                for side in range(2):
                    t = 2 * p + side
                    for a, b in ((0, HB), (HB, D)) if t == B - 1 else ((0, D),):
                        sp.wait_ge(y_ready, t + 1 + a // HB)
                        sp.dma_start(out[t, :, a:b], y[:, y_slot(t), a:b]).then_inc(stored[side], 16)
            sp.wait_ge(stored[0], 16 * PAIRS)
            sp.wait_ge(stored[1], 16 * (PAIRS + 1))

        @block.gpsimd
        def _(pool):
            pool.memset(ident[:, :], 0.0).then_inc(const_step, 1)
            pool.memset(diag[:, :], 0.0).then_inc(const_step, 1)
            pool.wait_ge(const_step, 1)
            pool.affine_select(out=ident[:, :], in_=ident[:, :], compare_op=ALU.not_equal, fill=1.0, base=0,
                               pattern=[[-1, P]], channel_multiplier=1).then_inc(const_step, 1)
            pool.wait_ge(const_step, 2)
            pool.affine_select(out=diag[:, :], in_=diag[:, :], compare_op=ALU.not_equal, fill=1.0, base=SIDE + KC - 1,
                               pattern=[[-1, NCAT + KC - 1]], channel_multiplier=KC).then_inc(const_step, 1)
            pool.iota(expert_no[:, :], pattern=[[1, E]], base=0, channel_multiplier=0,
                      allow_small_or_imprecise_dtypes=True).then_inc(const_step, 1)
            pool.memset(u0[:, :, R0:U0], 1.0).then_inc(const_step, 1)

            def place_a0(t, side):
                pool.wait_ge(a0_gathered[t // 2], 16 * 2)
                pool.tensor_copy(m0[side][:, :, SIDE:N0], lora_a0_g[:, t, :, :]).then_inc(a0_placed, 1)

            def place_next_a0(p):
                for side in range(2):
                    t = 2 * p + side
                    pool.wait_ge(l0_scored, t - 1)
                    place_a0(t, side)

            def place_a1(t, side):
                at = A1_AT[side]
                src = lora1_g[:, t, 0, :, :]
                pool.tensor_copy(m1_b[HIGH][:, :, at:at + R1], src).then_inc(a1_high, 1)
                pool.wait_ge(a1_high, t + 1)
                pool.tensor_tensor(m1_b[LOW][:, :, at:at + R1], src,
                                   m1_b[HIGH][:, :, at:at + R1].bitcast(F32), ALU.subtract).then_inc(a1_placed, 1)

            def low(dst, exact, high):
                return pool.tensor_tensor(dst, exact, high.bitcast(F32), ALU.subtract)

            def low_m1(c, n):
                a, b = BLOCKS[n]
                pool.wait_ge(*high_of(F_M1[c][n]))
                m1 = [m[:, c, R1:R1 + NB] for m in m1_b] if n == 0 else [m[:, c, :] for m in m1_a]
                low(m1[LOW], m1_f[:, c % 2, a:b], m1[HIGH]).then_inc(m1_low, 1)

            place_a0(0, 0)
            place_a0(1, 1)
            pool.wait_ge(exp_b0_high, 1)
            low(exp_b0_s[LOW][:, :, :].rearrange("p c n -> p (c n)"), exp_b_n[:, 0, :],
                exp_b0_s[HIGH][:, :, :].rearrange("p c n -> p (c n)")).then_inc(exp_b0_low, 1)
            for c in range(FIRST):
                low_m1(c, 0)
                low_m1(c, 1)
            low_m1(2, 0)
            pool.wait_ge(lora1_gathered, 16 * B)
            place_a1(0, 0)
            place_a1(1, 1)
            low_m1(2, 1)
            place_next_a0(1)
            low_m1(3, 0)
            low_m1(3, 1)
            for p in range(1, PAIRS):
                if p > 1:
                    place_next_a0(p)
                for side in range(2):
                    t = 2 * p + side
                    pool.wait_ge(side_scored, t - 1)
                    place_a1(t, side)

        @block.tensor
        def _(pe):
            def turn(dst, src, start=True):
                return pe.matmul(dst, src, ident[:, :], start=start, stop=True, is_transpose=True,
                                 skip_group_check=True)

            def products(dst, left, right, start, stop, low_left=None):
                for n, (a, b) in enumerate(PASSES):
                    if a == LOW and low_left:
                        pe.wait_ge(*low_left)
                    last = pe.matmul(dst, left[a], right[b], start=start and n == 0, stop=stop and n == 2,
                                     skip_group_check=True)
                return last

            def fill(n):
                before = [k for k in range(n) if BANK_OF[k] == BANK_OF[n]]
                if before:
                    pe.wait_ge(*emptied(before[-1]))
                return banks[BANK_OF[n]]

            def multiply_w1(c, n, chunks=range(KC)):
                a, b = BLOCKS[n]
                bank = fill(F_M1[c][n]) if chunks[0] == 0 else banks[BANK_OF[F_M1[c][n]]]
                at = NCAT + c * P
                for k in chunks:
                    last = products(bank[:, 0:b - a], [t[:, k, at:at + P] for t in cat1_w1_s],
                                    [t[:, k, a:b] for t in cat1_w1_s], k == 0, k == KC - 1)
                if chunks[-1] == KC - 1:
                    last.then_inc(prep_filled, 1)

            def multiply_w0(k):
                pe.wait_ge(w0_cat0_in[k], 16)
                side0 = w0_cat0_n[:, k, D:D + SIDE]
                for n, chunks in ((F_M0, range(KC - 1)), (F_M0_G0, range(KC - 1, KC))):
                    bank = banks[BANK_OF[n]]
                    for c in chunks:
                        at = (c - chunks[0]) * SIDE
                        last = pe.matmul(bank[:, at:at + SIDE], w0_cat0_n[:, k, c:D:KC], side0,
                                         start=k == 0 and at == 0, stop=k == KC - 1, skip_group_check=True)
                    if n == F_M0_G0 and k == KC - 1:
                        for j in range(KC):
                            last = pe.matmul(bank[0:U0, SIDE:2 * SIDE], w0_cat0_n[:, j, D + SIDE:D + SIDE + U0],
                                             w0_cat0_n[:, j, D:D + SIDE], start=j == 0, stop=j == KC - 1,
                                             skip_group_check=True)
                    if k == KC - 1:
                        last.then_inc(prep_filled, 1)

            def multiply_first_w1(k):
                pe.wait_ge(cat1_w1_low, k + 1)
                for c in range(FIRST):
                    multiply_w1(c, 0, range(k, k + 1))
                    multiply_w1(c, 1, range(k, k + 1))

            def multiply_lora_b1(n):
                pe.wait_ge(lora_b1_low, 1)
                a, b = BLOCKS[n]
                bank = fill(F_G1 + n)
                for k in range(KC):
                    last = products(bank[:, 0:b - a], [t[:, k, :, :].rearrange("p r b -> p (r b)") for t in lora_b1_s],
                                    [t[:, k, a:b] for t in cat1_w1_s], k == 0, k == KC - 1)
                last.then_inc(prep_filled, 1)

            def score0(q, side):
                t = 2 * q + side
                if side == 0:
                    pe.wait_ge(x_loaded, 16 * (q + 1))
                pe.wait_ge(a0_placed, t + 1)
                if q > 0 and side == 1:
                    pe.wait_ge(x1_summed, 2 * q)
                for c in range(KC):
                    last = pe.matmul(bank_l0[side][:, 0:N0], x_t[q % 2][:, c, side, :], m0[side][:, c, :],
                                     start=c == 0, stop=c == KC - 1, skip_group_check=True)
                last.then_inc(l0_scored, 1)

            def turn_u0(q, side):
                pe.wait_ge(u0_copied, 2 * q + side + 1)
                turn(bank_l0[side][0:U0, U0_T:U0_T + P], u0[:, side, :], start=False).then_inc(u0t_filled, 1)

            def adapt0(q, side):
                pe.wait_ge(u0t_copied, 2 * q + side + 1)
                pe.matmul(bank_l0[side][:, 0:SIDE], u0_t[:, side, :], g0[:, :], start=False, stop=True,
                          skip_group_check=True).then_inc(l0_ready, 1)

            def turn_gated0(q, side):
                pe.wait_ge(gated0_ready, 2 * q + side + 1)
                turn(bank_l0[side][:, GATED0_T:GATED0_T + P], gated0[:, side, :], start=False
                     ).then_inc(gated0t_filled, 1)

            def ffn0(q):
                pe.wait_ge(gated0t_low, 2 * q + 2)
                for r, bank in enumerate((bank_x1_u1, bank_l0[1])):
                    for j in range(2):
                        c = 2 * r + j
                        last = products(bank[:, j * 2 * P:(j + 1) * 2 * P], [w[:, c, :] for w in exp_b0_s],
                                        [g[:, :, :] for g in gated0_t], True, True)
                    last.then_inc(x1_filled, 1)

            def side1(p, side, chunks):
                t = 2 * p + side
                if chunks[0] == 0:
                    pe.wait_ge(a1_placed, t + 1)
                    if 0 < p and t < B - 1:
                        pe.wait_ge(y_ready, t - 1)
                a = 0 if side == 0 else R1
                for c in chunks:
                    if side == 0:
                        pe.wait_ge(x1_high, 2 * p + c // 2 + 1)
                    if t == 0:
                        pe.wait_ge(m1_low, 2 * c + 1)
                    last = products(acc_of(2 * p + side)[:, 0:R1 + NB], [v[:, c, side, :] for v in x1_t[p % 2]],
                                    [m[:, c, a:a + R1 + NB] for m in m1_b], c == 0, c == KC - 1,
                                    (x1_low, 2 * p + c // 2 + 1))
                if chunks[-1] == KC - 1:
                    last.then_inc(side_scored, 1)

            def base1(p, side, chunks):
                if p == 0 and side == 0 and chunks[-1] == KC - 1:
                    pe.wait_ge(m1_low, 2 * KC)
                for c in chunks:
                    products(acc_of(2 * p + side)[:, 512:512 + HB], [v[:, c, side, :] for v in x1_t[p % 2]],
                             [m[:, c, :] for m in m1_a], c == 0, False)

            def turn_u1(p, side):
                pe.wait_ge(u1_copied, 2 * p + side + 1)
                turn(bank_x1_u1[0:U1, side * P:(side + 1) * P], u1[:, side, :, :]).then_inc(u1t_filled, 1)

            def adapt_side1(p, side):
                pe.wait_ge(u1t_low, 2 * p + side + 1)
                at = SIDE_AT[side]
                pe.matmul(acc_of(2 * p + side)[:, at:at + NB], u1_t[:, side, :], g1_stack[:, 2 * p + side, 0:NB],
                          start=False, stop=False, skip_group_check=True).then_inc(l1_ready, 1)

            def adapt_base1(p, side):
                pe.matmul(acc_of(2 * p + side)[:, 512:512 + HB], u1_t[:, side, :], g1_stack[:, 2 * p + side, NB:NCAT],
                          start=False, stop=False, skip_group_check=True)

            def turn_gated1(p, side):
                pe.wait_ge(gated1_ready, 2 * p + side + 1)
                turn(bank_gated1[:, side * P:(side + 1) * P], gated1[:, side, :]).then_inc(gated1t_filled, 1)

            def ffn1(p, side):
                if p == 0 and side == 0:
                    pe.wait_ge(exp_b1_low, 1)
                pe.wait_ge(gated1t_high, 2 * p + side + 1)
                low_left = (gated1t_low, 2 * p + side + 1)
                left = [g[:, side, :] for g in gated1_t]
                at = SIDE_AT[side] + SIDE
                last = products(acc_of(2 * p + side)[:, at:at + HB], left, [e[:, 0:HB] for e in exp_b1_s], False, True,
                                low_left)
                if 2 * p + side == B - 1:
                    last.then_inc(y_filled, 1)
                products(acc_of(2 * p + side)[:, 512:512 + HB], left, [e[:, HB:D] for e in exp_b1_s], False, True
                         ).then_inc(y_filled, 1)

            for k in range(KC):
                multiply_w0(k)
            multiply_first_w1(0)
            pe.wait_ge(m0_copied, 1)
            score0(0, 0)
            score0(0, 1)
            multiply_first_w1(1)
            pe.wait_ge(const_step, 6)
            turn_u0(0, 0)
            turn_u0(0, 1)
            multiply_first_w1(2)
            adapt0(0, 0)
            adapt0(0, 1)
            multiply_first_w1(3)
            pe.wait_ge(cat1_w1_low, KC + 1)
            multiply_w1(2, 0, range(KC - 1))
            turn_gated0(0, 0)
            turn_gated0(0, 1)
            multiply_w1(2, 0, range(KC - 1, KC))
            multiply_w1(2, 1)
            pe.wait_ge(exp_b0_low, 1)
            ffn0(0)
            multiply_lora_b1(0)
            multiply_lora_b1(1)
            pe.wait_ge(*low_of(F_M1[2][1]))
            side1(0, 0, range(KC - 1))
            multiply_w1(3, 0)
            multiply_w1(3, 1)
            early, late = range(KC // 2), range(KC // 2, KC)
            for p in range(PAIRS - 1):
                q = p + 1
                score0(q, 0)
                side1(p, 0, range(KC) if p > 0 else range(KC - 1, KC))
                if p > 0:
                    turn_gated1(p - 1, 1)
                score0(q, 1)
                turn_u1(p, 0)
                if p > 0:
                    ffn1(p - 1, 1)
                else:
                    pe.wait_ge(*low_of(F_M1[3][1]))
                    side1(p, 1, early)
                    pe.wait_ge(g1_stacked, 16 * len(PASSES))
                turn_u0(q, 0)
                turn_u0(q, 1)
                adapt_side1(p, 0)
                if p > 0:
                    base1(p, 0, early)
                else:
                    side1(p, 1, range(KC // 2, KC - 1))
                adapt0(q, 0)
                adapt0(q, 1)
                side1(p, 1, range(KC) if p > 0 else range(KC - 1, KC))
                turn_gated1(p, 0)
                base1(p, 0, late if p > 0 else range(KC))
                turn_u1(p, 1)
                turn_gated0(q, 0)
                turn_gated0(q, 1)
                adapt_base1(p, 0)
                ffn1(p, 0)
                adapt_side1(p, 1)
                if q < PAIRS - 1:
                    base1(p, 1, early)
                    ffn0(q)
                    base1(p, 1, late)
                else:
                    ffn0(q)
                    base1(p, 1, range(KC))
                adapt_base1(p, 1)
            p = PAIRS - 1
            side1(p, 0, range(KC))
            side1(p, 1, range(1))
            turn_gated1(p - 1, 1)
            turn_u1(p, 0)
            side1(p, 1, range(1, KC // 2))
            ffn1(p - 1, 1)
            adapt_side1(p, 0)
            side1(p, 1, late)
            base1(p, 0, early)
            turn_u1(p, 1)
            base1(p, 0, late)
            adapt_base1(p, 0)
            turn_gated1(p, 0)
            adapt_side1(p, 1)
            base1(p, 1, early)
            ffn1(p, 0)
            base1(p, 1, late)
            adapt_base1(p, 1)
            turn_gated1(p, 1)
            ffn1(p, 1)

        @block.scalar
        def _(act):
            def blocks(n, count, w):
                return banks[BANK_OF[n]][:, 0:count * w].rearrange("p (k w) -> p k w", k=count)

            def copy(dst, src, **more):
                return act.activation(dst, src, ACT.Copy, **more)

            def filled(n):
                act.wait_ge(prep_filled, n + 1)

            def high_m1(c, n):
                a, b = BLOCKS[n]
                act.wait_ge(*low_of(F_M1[c][n]))
                copy(m1_b[HIGH][:, c, R1:R1 + NB] if n == 0 else m1_a[HIGH][:, c, :], m1_f[:, c % 2, a:b]
                     ).then_inc(prep_high, 1)

            def copy_u0(q, side):
                act.wait_ge(l0_scored, 2 * q + side + 1)
                copy(u0[:, side, 0:R0], bank_l0[side][:, SIDE:N0], scale=SCALE0).then_inc(u0_copied, 1)

            def copy_u0t(q, side):
                act.wait_ge(u0t_filled, 2 * q + side + 1)
                copy(u0_t[:, side, :], bank_l0[side][0:U0, U0_T:U0_T + P]).then_inc(u0t_copied, 1)

            def high_gated0(q, side):
                act.wait_ge(gated0t_filled, 2 * q + side + 1)
                copy(gated0_t[HIGH][:, side, :], bank_l0[side][:, GATED0_T:GATED0_T + P]).then_inc(gated0t_high, 1)

            def high_x1(q, r):
                act.wait_ge(x1_summed, 2 * q + r + 1)
                copy(x1_t[q % 2][HIGH][:, 2 * r:2 * r + 2, :, :], x1_f[:, 2 * r:2 * r + 2, :, :]).then_inc(x1_high, 1)

            def copy_u1(p, side):
                act.wait_ge(side_scored, 2 * p + side + 1)
                at = U1_AT[side]
                copy(u1[:, side, :, :], acc_of(2 * p + side)[:, at:at + R1].unsqueeze(1).to_broadcast([P, len(PASSES), R1])
                     ).then_inc(u1_copied, 1)

            def high_u1(p, side):
                act.wait_ge(u1t_filled, 2 * p + side + 1)
                copy(u1_t[:, side, :], bank_x1_u1[0:U1, side * P:(side + 1) * P]).then_inc(u1t_high, 1)

            def exp1(p, side):
                act.wait_ge(below_ready, 2 * p + side + 1)
                act.activation(expo[:, side, :], below[:, side, :], ACT.Exp).then_inc(expo_ready, 1)

            def high_gated1(p, side):
                act.wait_ge(gated1t_filled, 2 * p + side + 1)
                copy(gated1_t[HIGH][:, side, :], bank_gated1[:, side * P:(side + 1) * P]).then_inc(gated1t_high, 1)

            def high_first(k):
                act.wait_ge(cat1_w1_in[k], 16)
                copy(cat1_w1_s[HIGH][:, k, 0:NFIRST], cat1_w1_n[:, k, 0:NFIRST]).then_inc(cat1_w1_high, 1)

            high_first(0)
            filled(F_M0)
            copy(m0[0][:, 0:KC - 1, 0:SIDE], blocks(F_M0, KC - 1, SIDE)).then_inc(prep_high, 1)
            filled(F_M0_G0)
            copy(m0[0][:, KC - 1, 0:SIDE], banks[BANK_OF[F_M0_G0]][:, 0:SIDE])
            copy(g0[:, :], banks[BANK_OF[F_M0_G0]][0:U0, SIDE:2 * SIDE]).then_inc(prep_high, 1)
            high_first(1)
            high_first(2)
            copy_u0(0, 0)
            copy_u0(0, 1)
            high_first(3)
            copy_u0t(0, 0)
            copy_u0t(0, 1)
            act.wait_ge(w1_rest_in, 16)
            copy(cat1_w1_s[HIGH][:, :, NFIRST:NW], cat1_w1_n[:, :, NFIRST:NW]).then_inc(cat1_w1_high, 1)
            act.wait_ge(exp_b_in, 16)
            copy(exp_b0_s[HIGH][:, :, :].rearrange("p c n -> p (c n)"), exp_b_n[:, 0, :]).then_inc(exp_b0_high, 1)
            high_m1(0, 0)
            high_m1(0, 1)
            high_m1(1, 0)
            high_m1(1, 1)
            high_gated0(0, 0)
            high_gated0(0, 1)
            act.wait_ge(lora1_gathered, 16 * B)
            copy(lora_b1_s[HIGH][:, :, :, :], lora1_g[:, :, 1, :, :].rearrange("p b c r -> p c r b")
                 ).then_inc(lora_b1_high, 1)
            high_m1(2, 0)
            high_x1(0, 0)
            high_x1(0, 1)
            high_m1(2, 1)
            for n, (a, b) in enumerate(BLOCKS):
                filled(F_G1 + n)
                copy(g1[HIGH][:, a:b], banks[BANK_OF[F_G1 + n]][:, 0:b - a]).then_inc(prep_high, 1)
            copy(exp_b1_s[HIGH][:, :], exp_b_n[:, 1, :], scale=SCALE_FFN1).then_inc(exp_b1_high, 1)
            high_m1(3, 0)
            high_m1(3, 1)
            for p in range(PAIRS - 1):
                q = p + 1
                copy_u0(q, 0)
                copy_u1(p, 0)
                if p > 0:
                    high_gated1(p - 1, 1)
                copy_u0(q, 1)
                high_u1(p, 0)
                copy_u0t(q, 0)
                copy_u0t(q, 1)
                exp1(p, 0)
                copy_u1(p, 1)
                high_gated1(p, 0)
                high_u1(p, 1)
                high_gated0(q, 0)
                high_gated0(q, 1)
                high_x1(q, 0)
                high_x1(q, 1)
                exp1(p, 1)
            p = PAIRS - 1
            copy_u1(p, 0)
            high_gated1(p - 1, 1)
            high_u1(p, 0)
            exp1(p, 0)
            copy_u1(p, 1)
            high_u1(p, 1)
            high_gated1(p, 0)
            exp1(p, 1)
            high_gated1(p, 1)

        @block.vector
        def _(dve):
            def blocks(n, count, w):
                return banks[BANK_OF[n]][:, 0:count * w].rearrange("p (k w) -> p k w", k=count)

            def low(dst, exact, high):
                return dve.tensor_tensor(dst, exact, high.bitcast(F32), ALU.subtract)

            steps = [0]

            def finished(ins):
                steps[0] += 1
                ins.then_inc(dve_step, 1)
                dve.wait_ge(dve_step, steps[0])

            def low_w1(n, chunks, a, b):
                dve.wait_ge(cat1_w1_high, n + 1)
                low(cat1_w1_s[LOW][:, chunks, a:b], cat1_w1_n[:, chunks, a:b], cat1_w1_s[HIGH][:, chunks, a:b]
                    ).then_inc(cat1_w1_low, 1)

            def sum_m1(c, n):
                if c >= 2:
                    dve.wait_ge(*high_of(F_M1[c - 2][n]))
                    dve.wait_ge(m1_low, 2 * (c - 2) + n + 1)
                a, b = BLOCKS[n]
                at = KC - 1 - c
                dve.wait_ge(prep_filled, F_M1[c][n] + 1)
                dve.tensor_tensor(m1_f[:, c % 2, a:b], banks[BANK_OF[F_M1[c][n]]][:, 0:b - a],
                                  diag[:, at + a:at + b], ALU.add).then_inc(prep_low, 1)

            def route0(q, side):
                scores = bank_l0[side][:, ER:SIDE]
                dve.wait_ge(l0_ready, 2 * q + side + 1)
                finished(dve.max(top0[:, side, :], scores))
                finished(dve.max_index(top0_at[:, side, :], top0[:, side, :], scores))
                finished(dve.scalar_tensor_tensor(out=gate0[:, side, :], in0=expert_no[:, :], scalar=top0_at[:, side, 0:1],
                                                  in1=scores, op0=ALU.is_equal, op1=ALU.mult))
                dve.tensor_tensor(gated0[:, side, :].rearrange("p (e r) -> p e r", e=E),
                                  bank_l0[side][:, 0:ER].rearrange("p (e r) -> p e r", e=E),
                                  gate0[:, side, :].unsqueeze(2).to_broadcast([P, E, RE]), ALU.mult
                                  ).then_inc(gated0_ready, 1)

            def low_gated0(q, side):
                dve.wait_ge(gated0t_high, 2 * q + side + 1)
                low(gated0_t[LOW][:, side, :], bank_l0[side][:, GATED0_T:GATED0_T + P], gated0_t[HIGH][:, side, :]
                    ).then_inc(gated0t_low, 1)

            def sum_x1(q, r):
                dve.wait_ge(x1_filled, 2 * q + r + 1)
                dve.tensor_tensor(x1_f[:, 2 * r:2 * r + 2, :, :],
                                  (bank_x1_u1[:, :], bank_l0[1])[r].rearrange("p (c s t) -> p c s t", c=2, s=2),
                                  x_t[q % 2][:, 2 * r:2 * r + 2, :, :], ALU.add).then_inc(x1_summed, 1)

            def low_x1(q, r):
                dve.wait_ge(x1_high, 2 * q + r + 1)
                low(x1_t[q % 2][LOW][:, 2 * r:2 * r + 2, :, :], x1_f[:, 2 * r:2 * r + 2, :, :],
                    x1_t[q % 2][HIGH][:, 2 * r:2 * r + 2, :, :]).then_inc(x1_low, 1)

            def low_u1(p, side):
                dve.wait_ge(u1t_high, 2 * p + side + 1)
                low(u1_t[2 * R1:U1, side, :], bank_x1_u1[2 * R1:U1, side * P:(side + 1) * P], u1_t[2 * R1:U1, side, :]
                    ).then_inc(u1t_low, 1)

            def route1(p, side):
                t = 2 * p + side
                at = SIDE_AT[side]
                scores = acc_of(2 * p + side)[:, at + ER:at + SIDE]
                dve.wait_ge(l1_ready, t + 1)
                finished(dve.max(top1[:, side, :], scores))
                dve.tensor_scalar(below[:, side, :], scores, top1[:, side, 0:1], None, ALU.subtract).then_inc(below_ready, 1)
                finished(dve.max_index(top1_at[:, side, :], top1[:, side, :], scores))
                finished(dve.tensor_scalar(first[:, side, :], expert_no[:, :], top1_at[:, side, 0:1], None, ALU.is_equal))
                finished(dve.scalar_tensor_tensor(out=chosen[:, side, :], in0=expert_no[:, :], scalar=top1_at[:, side, 1:2],
                                                  in1=first[:, side, :], op0=ALU.is_equal, op1=ALU.add))
                dve.wait_ge(expo_ready, t + 1)
                finished(dve.scalar_tensor_tensor(out=weight[:, side, :], in0=chosen[:, side, :], scalar=1.0,
                                                  in1=expo[:, side, :], op0=ALU.mult, op1=ALU.mult,
                                                  accum_out=total[:, side:side + 1]))
                finished(dve.reciprocal(inverse[:, side:side + 1], total[:, side:side + 1]))
                dve.scalar_tensor_tensor(out=gated1[:, side, :].rearrange("p (e r) -> p e r", e=E),
                                         in0=acc_of(2 * p + side)[:, at:at + ER].rearrange("p (e r) -> p e r", e=E),
                                         scalar=inverse[:, side:side + 1],
                                         in1=weight[:, side, :].unsqueeze(2).to_broadcast([P, E, RE]),
                                         op0=ALU.mult, op1=ALU.mult).then_inc(gated1_ready, 1)

            def low_gated1(p, side):
                dve.wait_ge(gated1t_high, 2 * p + side + 1)
                low(gated1_t[LOW][:, side, :], bank_gated1[:, side * P:(side + 1) * P], gated1_t[HIGH][:, side, :]
                    ).then_inc(gated1t_low, 1)

            def sum_y(p, side):
                t = 2 * p + side
                if t == B - 1:
                    for h in range(2):
                        dve.wait_ge(y_filled, t + 1 + h)
                        dve.tensor_tensor(y[:, y_slot(t), h * HB:(h + 1) * HB], base_part(t)[:, h, :],
                                          b_base_all[:, h * HB:(h + 1) * HB], ALU.add).then_inc(y_ready, 1)
                    return
                dve.wait_ge(y_filled, t + 1)
                if p > 0:
                    dve.wait_ge(stored[side], 16 * p)
                dve.tensor_tensor(y[:, side, :].rearrange("p (a b) -> p a b", a=2), base_part(t),
                                  b_base_all[:, :].rearrange("p (a b) -> p a b", a=2), ALU.add).then_inc(y_ready, 1)

            low_w1(0, 0, 0, NFIRST)
            dve.wait_ge(*high_of(F_M0_G0))
            dve.tensor_copy(m0[1][:, :, 0:SIDE], m0[0][:, :, 0:SIDE]).then_inc(m0_copied, 1)
            for k in range(1, KC):
                low_w1(k, k, 0, NFIRST)
            dve.wait_ge(const_step, 6)
            low_w1(KC, slice(0, KC), NFIRST, NW)
            sum_m1(0, 0)
            route0(0, 0)
            sum_m1(0, 1)
            route0(0, 1)
            sum_m1(1, 0)
            sum_m1(1, 1)
            low_gated0(0, 0)
            low_gated0(0, 1)
            dve.wait_ge(lora_b1_high, 1)
            low(lora_b1_s[LOW][:, :, :, :], lora1_g[:, :, 1, :, :].rearrange("p b c r -> p c r b"),
                lora_b1_s[HIGH][:, :, :, :]).then_inc(lora_b1_low, 1)
            sum_m1(2, 0)
            sum_x1(0, 0)
            sum_x1(0, 1)
            low_x1(0, 0)
            low_x1(0, 1)
            sum_m1(2, 1)
            for n, (a, b) in enumerate(BLOCKS):
                dve.wait_ge(*high_of(F_G1 + n))
                low(g1[LOW][:, a:b], banks[BANK_OF[F_G1 + n]][:, 0:b - a], g1[HIGH][:, a:b]).then_inc(prep_low, 1)
            dve.wait_ge(exp_b1_high, 1)
            dve.scalar_tensor_tensor(out=exp_b1_s[LOW][:, :], in0=exp_b_n[:, 1, :], scalar=SCALE_FFN1,
                                     in1=exp_b1_s[HIGH][:, :].bitcast(F32), op0=ALU.mult, op1=ALU.subtract
                                     ).then_inc(exp_b1_low, 1)
            sum_m1(3, 0)
            sum_m1(3, 1)
            dve.wait_ge(b_base_in, 16)
            for p in range(PAIRS - 1):
                q = p + 1
                if p > 0:
                    low_gated1(p - 1, 1)
                low_u1(p, 0)
                if p > 0:
                    sum_y(p - 1, 1)
                route1(p, 0)
                route0(q, 0)
                route0(q, 1)
                low_gated1(p, 0)
                low_u1(p, 1)
                low_gated0(q, 0)
                low_gated0(q, 1)
                sum_y(p, 0)
                sum_x1(q, 0)
                sum_x1(q, 1)
                low_x1(q, 0)
                low_x1(q, 1)
                route1(p, 1)
            p = PAIRS - 1
            low_gated1(p - 1, 1)
            low_u1(p, 0)
            route1(p, 0)
            low_u1(p, 1)
            low_gated1(p, 0)
            route1(p, 1)
            sum_y(p - 1, 1)
            low_gated1(p, 1)
            sum_y(p, 0)
            sum_y(p, 1)


def _lay_out(inputs):
    import numpy as np

    v = {name: np.asarray(a) for name, a in inputs.items()}
    d = v["x"].shape[2]
    kc = d // P

    def strided(a):
        return a.reshape(len(a), P, kc).transpose(1, 2, 0)

    def blocked(a):
        return a.reshape(len(a), kc, P).transpose(2, 1, 0)

    def rows(a):
        return a.reshape(-1, a.shape[2])

    w0_cat0 = np.concatenate([v["L0_cond_weight"].reshape(P, kc, d), strided(rows(v["L0_ffn_A"])),
                              strided(v["L0_ffn_route_w"]), v["L0_cond_lora_B"].reshape(P, kc, -1),
                              v["L0_cond_bias"].reshape(P, kc, 1)], axis=2)
    w1 = v["L1_cond_W"].reshape(P, kc, d).transpose(1, 0, 2).reshape(d, d)
    cat1_w1 = np.concatenate([blocked(rows(v["L1_ffn_A_stack"])), blocked(v["L1_ffn_W_router"]),
                              blocked(v["L1_ffn_W_base"]), blocked(w1)], axis=2)
    exp_b0, exp_b1 = (rows(v[n].transpose(0, 2, 1)) for n in ("L0_ffn_Bw", "L1_ffn_B_stack"))
    exp_b = np.stack([exp_b0.reshape(-1, P, kc).transpose(0, 2, 1).reshape(-1, d), exp_b1], axis=1)
    lora_a0 = v["L0_cond_lora_A"].reshape(-1, P, kc, v["L0_cond_lora_A"].shape[2])
    a1, b1 = v["L1_cond_lora_A"], v["L1_cond_lora_B"]
    lora1 = np.stack([a1.reshape(-1, P, kc, a1.shape[2]),
                      b1.reshape(len(b1), -1, kc, P).transpose(0, 3, 2, 1)], axis=2)
    x_turned = v["x"].reshape(-1, 2, v["x"].shape[1], P, kc).transpose(0, 3, 4, 1, 2)
    return {"x_turned": x_turned, "labels": np.stack([v["itok_B_0_4"], v["itok_B_0_15"]]), "w0_cat0": w0_cat0,
            "lora_a0": lora_a0, "exp_b": exp_b, "cat1_w1": cat1_w1, "lora1": lora1, "b_base": v["L1_ffn_b_base"]}


def kernel(**inputs):
    import numpy as _np
    import concourse.bacc as _bacc
    from concourse import mybir as _mybir
    from concourse.bass_utils import run_bass_kernel_spmd as _run

    nc = _bacc.Bacc("TRN2", target_bir_lowering=False, num_devices=1)
    arrays, args = {}, []
    for name, laid_out in _lay_out(inputs).items():
        a = _np.ascontiguousarray(laid_out)
        arrays[f"in_{name}_dram"] = a
        args.append(nc.dram_tensor(f"in_{name}_dram", a.shape, _mybir.dt.from_np(a.dtype), kind="ExternalInput").ap())
    out = nc.dram_tensor("out_0_dram", inputs["x"].shape, _mybir.dt.float32, kind="ExternalOutput").ap()
    adaln_ffn_kernel(nc, *args, out)
    r = _run(nc, [arrays], core_ids=[0])
    return r.results[0]["out_0_dram"]
```
